# Optimizing a Trainium2 kernel written in Bass

```python
import numpy as np
import jax
import jax.numpy as jnp

def _softmax(x, axis=-1):
    return jax.nn.softmax(x, axis=axis)

def _gelu(x):
    return jax.nn.gelu(x, approximate=True)

def _silu(x):
    return jax.nn.silu(x)

def _sigmoid(x):
    return jax.nn.sigmoid(x)

def _layernorm(x, axis=-1, eps=1e-05):
    m = jnp.mean(x, axis=axis, keepdims=True)
    v = jnp.var(x, axis=axis, keepdims=True)
    return (x - m) / jnp.sqrt(v + eps)

def _scatter_add(tgt, idx, src, axis=0):
    return tgt.at[idx].add(src)

def _segment_sum(src, seg, n):
    return jax.ops.segment_sum(src, seg, n)
kernel_name = 'mk_xattn_ffn_d2_seqx_r8_c8fb27'

def setup_inputs(seed: int=0):
    np.random.seed(seed)
    _w = jnp.asarray

    def _rec_inputs():
        import jax
        import jax.numpy as jnp
        _rk = jax.random.key(seed)
        x = 7.22e-05 + 1 * jax.random.normal(jax.random.fold_in(_rk, 1), (64, 128, 128), jnp.float32)
        _lenS = 128 - jax.random.randint(jax.random.fold_in(_rk, 7), (64,), 0, max(1, 128 // 4) + 1, jnp.int32)
        _lenS2 = 120 - jax.random.randint(jax.random.fold_in(_rk, 8), (64,), 0, max(1, 120 // 4) + 1, jnp.int32)
        _ctx_1024P = jax.random.normal(jax.random.fold_in(_rk, 11), (64, 16, 128), jnp.float32)
        _ctx_1024c = jax.random.dirichlet(jax.random.fold_in(_rk, 511), 0.3 * jnp.ones((16,), jnp.float32), (64, 120))
        _ctx_1024t = jnp.einsum('bsk,bkd->bsd', _ctx_1024c, _ctx_1024P)
        _ctx_1024t = _ctx_1024t * jax.lax.rsqrt(jnp.mean(jnp.square(_ctx_1024t)) + 1e-12) * 0.953939
        ctx_1024 = 4.13588e-05 + 0.999923 * (_ctx_1024t + 0.3 * jax.random.normal(jax.random.fold_in(_rk, 611), (64, 120, 128), jnp.float32))
        return (x, ctx_1024)
    x, ctx_1024 = _rec_inputs()

    def _L0_xattn_setup():
        import jax, jax.numpy as jnp
        import numpy as np
        D = 128
        H = 16
        HD = D // H
        EPS = 1e-06

        def rms_norm(x, w):
            xf = x.astype(jnp.float32)
            rms = jnp.sqrt(jnp.mean(xf * xf, axis=-1, keepdims=True) + EPS)
            return (xf / rms * w.astype(jnp.float32)).astype(x.dtype)
        key = jax.random.key(seed)
        ks = jax.random.split(key, 10)
        B, S, Sc = (4, 256, 256)
        s = 0.02
        return {'x': jax.random.normal(ks[0], (B, S, D), jnp.float32), 'ctx': jax.random.normal(ks[1], (B, Sc, D), jnp.float32), 'Wq': jax.random.normal(ks[2], (D, D), jnp.float32) * s, 'bq': jnp.zeros((D,), jnp.float32), 'Wkv': jax.random.normal(ks[3], (D, 2 * D), jnp.float32) * s, 'bkv': jnp.zeros((2 * D,), jnp.float32), 'Wproj': jax.random.normal(ks[4], (D, D), jnp.float32) * s, 'bproj': jnp.zeros((D,), jnp.float32), 'gq': jnp.ones((HD,), jnp.float32), 'gk': jnp.ones((HD,), jnp.float32)}
    _L0_xattn_all = _L0_xattn_setup()
    _L0_xattn_in = {k: v for k, v in _L0_xattn_all.items() if k in ('Wq', 'bq', 'Wkv', 'bkv', 'Wproj', 'bproj', 'gq', 'gk')}
    del _L0_xattn_all

    def _L0_ffn_setup():
        import jax, jax.numpy as jnp
        import numpy as np
        B, S, D_MODEL, D_HIDDEN = (4, 256, 128, 512)

        def act_quant(x):
            scale = 127.0 / jnp.clip(jnp.max(jnp.abs(x), axis=-1, keepdims=True), 1e-05)
            return jnp.clip(jnp.round(x * scale), -128, 127) / scale

        def weight_quant(w):
            scale = 1.0 / jnp.clip(jnp.mean(jnp.abs(w)), 1e-05)
            return jnp.clip(jnp.round(w * scale), -1, 1) / scale

        def bit_linear(x, w):
            xq = x + jax.lax.stop_gradient(act_quant(x) - x)
            wq = w + jax.lax.stop_gradient(weight_quant(w) - w)
            return jnp.einsum('bsd,hd->bsh', xq, wq)

        def depthwise_conv1d(x_bcl, w, b):
            y = jax.lax.conv_general_dilated(x_bcl, w, window_strides=(1,), padding=[(1, 1)], dimension_numbers=('NCH', 'OIH', 'NCH'), feature_group_count=x_bcl.shape[1])
            return y + b[None, :, None]
        key = jax.random.key(seed)
        ks = jax.random.split(key, 5)
        lim1 = 1.0 / np.sqrt(D_MODEL)
        lim2 = 1.0 / np.sqrt(D_HIDDEN)
        limc = 1.0 / np.sqrt(3.0)
        return {'x': jax.random.normal(ks[0], (B, S, D_MODEL), dtype=jnp.float32), 'w1': jax.random.uniform(ks[1], (D_HIDDEN, D_MODEL), jnp.float32, -lim1, lim1), 'conv_w': jax.random.uniform(ks[2], (D_HIDDEN, 1, 3), jnp.float32, -limc, limc), 'conv_b': jax.random.uniform(ks[3], (D_HIDDEN,), jnp.float32, -limc, limc), 'w2': jax.random.uniform(ks[4], (D_MODEL, D_HIDDEN), jnp.float32, -lim2, lim2)}
    _L0_ffn_all = _L0_ffn_setup()
    _L0_ffn_in = {k: v for k, v in _L0_ffn_all.items() if k in ('w1', 'conv_w', 'conv_b', 'w2')}
    del _L0_ffn_all

    def _L1_xattn_setup():
        import jax, jax.numpy as jnp
        import numpy as np
        import math
        B, SQ, SK, DQ, DK = (16, 256, 256, 128, 128)
        key = jax.random.key(seed)
        ks = jax.random.split(key, 6)
        return {'bert_feature': jax.random.normal(ks[0], (B, SQ, DQ), dtype=jnp.float32), 'knowledge_feature': jax.random.normal(ks[1], (B, SK, DK), dtype=jnp.float32), 'w1_w': jax.random.normal(ks[2], (DK, DQ), dtype=jnp.float32) * 0.02, 'w1_b': jax.random.normal(ks[3], (DK,), dtype=jnp.float32) * 0.02, 'w2_w': jax.random.normal(ks[4], (DQ, DQ + DK), dtype=jnp.float32) * 0.02, 'w2_b': jax.random.normal(ks[5], (DQ,), dtype=jnp.float32) * 0.02}
    _L1_xattn_all = _L1_xattn_setup()
    _L1_xattn_in = {k: v for k, v in _L1_xattn_all.items() if k in ('w1_w', 'w1_b', 'w2_w', 'w2_b')}
    del _L1_xattn_all

    def _L1_ffn_setup():
        import jax, jax.numpy as jnp
        import numpy as np
        B, S, D = (4, 512, 128)
        E, I = (8, 256)
        CAPACITY = 2
        K = max(1, int(S / E * CAPACITY))
        key = jax.random.key(seed)
        k1, k2, k3, k4, k5 = jax.random.split(key, 5)
        x = jax.random.normal(k1, (B, S, D), dtype=jnp.float32)
        gate_w = jax.random.normal(k2, (D, E), dtype=jnp.float32) * 0.006
        Wg = jax.random.normal(k3, (E, D, I), dtype=jnp.float32) * 0.02
        Wu = jax.random.normal(k4, (E, D, I), dtype=jnp.float32) * 0.02
        Wd = jax.random.normal(k5, (E, I, D), dtype=jnp.float32) * 0.02
        return {'x': x, 'gate_w': gate_w, 'Wg': Wg, 'Wu': Wu, 'Wd': Wd}
    _L1_ffn_all = _L1_ffn_setup()
    _L1_ffn_in = {k: v for k, v in _L1_ffn_all.items() if k in ('gate_w', 'Wg', 'Wu', 'Wd')}
    del _L1_ffn_all
    return {'x': x, 'ctx_1024': ctx_1024, 'L0_xattn_Wq': _L0_xattn_in['Wq'], 'L0_xattn_bq': _L0_xattn_in['bq'], 'L0_xattn_Wkv': _L0_xattn_in['Wkv'], 'L0_xattn_bkv': _L0_xattn_in['bkv'], 'L0_xattn_Wproj': _L0_xattn_in['Wproj'], 'L0_xattn_bproj': _L0_xattn_in['bproj'], 'L0_xattn_gq': _L0_xattn_in['gq'], 'L0_xattn_gk': _L0_xattn_in['gk'], 'L0_ffn_w1': _L0_ffn_in['w1'], 'L0_ffn_conv_w': _L0_ffn_in['conv_w'], 'L0_ffn_conv_b': _L0_ffn_in['conv_b'], 'L0_ffn_w2': _L0_ffn_in['w2'], 'L1_xattn_w1_w': _L1_xattn_in['w1_w'], 'L1_xattn_w1_b': _L1_xattn_in['w1_b'], 'L1_xattn_w2_w': _L1_xattn_in['w2_w'], 'L1_xattn_w2_b': _L1_xattn_in['w2_b'], 'L1_ffn_gate_w': _L1_ffn_in['gate_w'], 'L1_ffn_Wg': _L1_ffn_in['Wg'], 'L1_ffn_Wu': _L1_ffn_in['Wu'], 'L1_ffn_Wd': _L1_ffn_in['Wd']}

def reference(x, ctx_1024, L0_xattn_Wq, L0_xattn_bq, L0_xattn_Wkv, L0_xattn_bkv, L0_xattn_Wproj, L0_xattn_bproj, L0_xattn_gq, L0_xattn_gk, L0_ffn_w1, L0_ffn_conv_w, L0_ffn_conv_b, L0_ffn_w2, L1_xattn_w1_w, L1_xattn_w1_b, L1_xattn_w2_w, L1_xattn_w2_b, L1_ffn_gate_w, L1_ffn_Wg, L1_ffn_Wu, L1_ffn_Wd):
    import jax
    import jax.numpy as jnp

    def _L0_xattn_ref(x, ctx, Wq, bq, Wkv, bkv, Wproj, bproj, gq, gk):
        import jax, jax.numpy as jnp
        import numpy as np
        D = 128
        H = 16
        HD = D // H
        EPS = 1e-06

        def rms_norm(x, w):
            xf = x.astype(jnp.float32)
            rms = jnp.sqrt(jnp.mean(xf * xf, axis=-1, keepdims=True) + EPS)
            return (xf / rms * w.astype(jnp.float32)).astype(x.dtype)
        B, S, _ = x.shape
        Sc = ctx.shape[1]
        q = (x @ Wq + bq).reshape(B, S, H, HD)
        q = rms_norm(q, gq).transpose(0, 2, 1, 3)
        kv = (ctx @ Wkv + bkv).reshape(B, Sc, 2, H, HD)
        k = rms_norm(kv[:, :, 0], gk).transpose(0, 2, 1, 3)
        v = kv[:, :, 1].transpose(0, 2, 1, 3)
        scale = 1.0 / jnp.sqrt(jnp.asarray(HD, q.dtype))
        scores = jnp.einsum('bhsd,bhtd->bhst', q, k) * scale
        attn = jax.nn.softmax(scores, axis=-1)
        out = jnp.einsum('bhst,bhtd->bhsd', attn, v)
        out = out.transpose(0, 2, 1, 3).reshape(B, S, D)
        return out @ Wproj + bproj

    def _L0_ffn_ref(x, w1, conv_w, conv_b, w2):
        import jax, jax.numpy as jnp
        import numpy as np
        B, S, D_MODEL, D_HIDDEN = (4, 256, 128, 512)

        def act_quant(x):
            scale = 127.0 / jnp.clip(jnp.max(jnp.abs(x), axis=-1, keepdims=True), 1e-05)
            return jnp.clip(jnp.round(x * scale), -128, 127) / scale

        def weight_quant(w):
            scale = 1.0 / jnp.clip(jnp.mean(jnp.abs(w)), 1e-05)
            return jnp.clip(jnp.round(w * scale), -1, 1) / scale

        def bit_linear(x, w):
            xq = x + jax.lax.stop_gradient(act_quant(x) - x)
            wq = w + jax.lax.stop_gradient(weight_quant(w) - w)
            return jnp.einsum('bsd,hd->bsh', xq, wq)

        def depthwise_conv1d(x_bcl, w, b):
            y = jax.lax.conv_general_dilated(x_bcl, w, window_strides=(1,), padding=[(1, 1)], dimension_numbers=('NCH', 'OIH', 'NCH'), feature_group_count=x_bcl.shape[1])
            return y + b[None, :, None]
        h = bit_linear(x, w1)
        h = depthwise_conv1d(h.transpose(0, 2, 1), conv_w, conv_b)
        h = h.transpose(0, 2, 1)
        h = jax.nn.silu(h)
        return bit_linear(h, w2)

    def _L1_xattn_ref(bert_feature, knowledge_feature, w1_w, w1_b, w2_w, w2_b):
        import jax, jax.numpy as jnp
        import numpy as np
        import math
        B, SQ, SK, DQ, DK = (16, 256, 256, 128, 128)
        d_k = knowledge_feature.shape[-1]
        bf = jnp.einsum('bqd,kd->bqk', bert_feature, w1_w) + w1_b
        scores = jnp.einsum('bqd,bkd->bqk', bf, knowledge_feature) / math.sqrt(d_k)
        attn = jax.nn.softmax(scores, axis=-1)
        output = jnp.einsum('bqk,bkd->bqd', attn, knowledge_feature)
        fused = jnp.concatenate([bert_feature, output], axis=-1)
        return jnp.einsum('bqf,of->bqo', fused, w2_w) + w2_b

    def _L1_ffn_ref(x, gate_w, Wg, Wu, Wd):
        import jax, jax.numpy as jnp
        import numpy as np
        B, S, D = (4, 512, 128)
        E, I = (8, 256)
        CAPACITY = 2
        K = max(1, int(S / E * CAPACITY))
        logits = jnp.einsum('bsd,de->bse', x, gate_w)
        affinity = jax.nn.softmax(logits, axis=-1)
        affinity_T = jnp.transpose(affinity, (0, 2, 1))
        gating, index = jax.lax.top_k(affinity_T, K)
        b_idx = jnp.arange(x.shape[0])[:, None, None]
        x_sel = x[b_idx, index]
        g = jnp.einsum('bekd,edi->beki', x_sel, Wg)
        u = jnp.einsum('bekd,edi->beki', x_sel, Wu)
        h = jax.nn.silu(g) * u
        out = jnp.einsum('beki,eid->bekd', h, Wd)
        contrib = out * gating[..., None]
        x_out = jnp.zeros_like(x).at[b_idx, index].add(contrib)
        return x_out
    x = x + _L0_xattn_ref(_layernorm(x, axis=-1), ctx_1024, L0_xattn_Wq, L0_xattn_bq, L0_xattn_Wkv, L0_xattn_bkv, L0_xattn_Wproj, L0_xattn_bproj, L0_xattn_gq, L0_xattn_gk)
    x = x + _L0_ffn_ref(_layernorm(x, axis=-1), L0_ffn_w1, L0_ffn_conv_w, L0_ffn_conv_b, L0_ffn_w2)
    x = x + _L1_xattn_ref(_layernorm(x, axis=-1), ctx_1024, L1_xattn_w1_w, L1_xattn_w1_b, L1_xattn_w2_w, L1_xattn_w2_b)
    x = x + _L1_ffn_ref(_layernorm(x, axis=-1), L1_ffn_gate_w, L1_ffn_Wg, L1_ffn_Wu, L1_ffn_Wd)
    return x

_drawn_inputs = setup_inputs


def setup_inputs(seed=0):
    import zlib

    import numpy as np

    out = dict(_drawn_inputs(seed))
    spreads = {'L0_xattn_bq': (0.0, 2.0),
     'L0_xattn_bkv': (0.0, 0.389),
     'L0_xattn_bproj': (0.0, 0.1),
     'L0_xattn_gq': (1.0, 0.6),
     'L0_xattn_gk': (1.0, 0.6)}
    factors = {'L0_xattn_Wq': 35.714,
     'L1_xattn_w1_w': 5.941,
     'L1_xattn_w1_b': 34.056,
     'L1_ffn_gate_w': 8.0,
     'L1_ffn_Wg': 8.0,
     'L1_ffn_Wu': 8.0,
     'L1_ffn_Wd': 8.0}
    for name, (base, spread) in spreads.items():
        noise = np.random.default_rng([zlib.crc32(name.encode()), seed]).standard_normal(out[name].shape)
        drawn = base * np.exp(spread * noise) if base else spread * noise
        out[name] = jnp.asarray(drawn.astype(out[name].dtype))
    for name, factor in factors.items():
        out[name] = (out[name] * factor).astype(out[name].dtype)
    return out
```

```python
from contextlib import ExitStack

import concourse.bass as bass
from concourse import mybir

F32 = mybir.dt.float32
F16 = mybir.dt.float16
BF16 = mybir.dt.bfloat16
I32 = mybir.dt.int32
ALU = mybir.AluOpType
ACT = mybir.ActivationFunctionType
AX = mybir.AxisListType

B, S, SC, D = 64, 128, 120, 128
GB = 4
NG = B // GB
T = GB * S
H = 16
HD = D // H
HQ = 4
NQ = H // HQ
HID = 512
KB = HID // 128
E, I = 8, 256
NU = E * I // 128
EPS_LN, EPS_RMS, CLIP = 1e-5, 1e-6, 1e-5
MAGIC = 12582912.0
RSQRT_SEED = 1597463007.0
WSCALE = 64.0
LINKS_A, LINKS_B = 33, 76


class Signal:

    def __init__(self, sem, per):
        self.sem, self.per = sem, per

    def at(self, g, k=1):
        return g * self.per + k


def build_program(nc, x, ctx, ctx_t, wq, bq, wkv, bkv, wproj, bproj, gq, gk, w1t, conv_w, conv_b,
                  w2t, aw1t, aw1b, aw2t, aw2b, gate, wg, wu, wd, ident, head_mask, out):
    stack = ExitStack()
    with stack:
        def sb(name, shape, dt=F32):
            return stack.enter_context(nc.sbuf_tensor(name, shape, dt))

        def signal(name, per=1):
            return Signal(stack.enter_context(nc.semaphore(name)), per)

        wq_s, wk_s, wv_s, wp_s = (sb(n, [128, D]) for n in ("wq_s", "wk_s", "wv_s", "wp_s"))
        bq_s, bk_s, bv_s, bp_s, a2b_s = (sb(n, [128, D]) for n in ("bq_s", "bk_s", "bv_s", "bp_s", "a2b_s"))
        gq_s, gk_s, gg_s = (sb(n, [128, HD]) for n in ("gq_s", "gk_s", "gg_s"))
        w1_f, w2_f = sb("w1_f", [128, HID]), sb("w2_f", [128, KB, D])
        w1_i, w2_i = sb("w1_i", [128, HID], BF16), sb("w2_i", [128, KB, D], BF16)
        wabs = sb("wabs", [128, 2])
        wmean = sb("wmean", [128, 2])
        winv = sb("winv", [128, 2])
        cw_s, cb_s = sb("cw_s", [128, KB, 3]), sb("cb_s", [128, KB])
        aw1_s, aw1b_s, aw2_s = sb("aw1_s", [128, D]), sb("aw1b_s", [128, 1]), sb("aw2_s", [128, 2, D])
        gate_f = sb("gate_f", [128, E])
        gate_h, gate_l = sb("gate_h", [128, E], F16), sb("gate_l", [128, E], F16)
        w_stage = sb("w_stage", [128, E * I])
        wg_h, wg_l, wu_h, wu_l = (sb(n, [128, E * I], F16) for n in ("wg_h", "wg_l", "wu_h", "wu_l"))
        wd_s = sb("wd_s", [128, NU, D])
        id_f, id_h, id_b = sb("id_f", [128, 128]), sb("id_h", [128, 128], F16), sb("id_b", [128, 128], BF16)
        mask_f, mask_h = sb("mask_f", [128, H]), sb("mask_h", [128, H], F16)
        ones = sb("ones", [128, 128])
        magic = sb("magic", [128, 1])

        xin, xres, xres_b = (sb(n, [128, GB, D]) for n in ("xin", "xres", "xres_b"))
        ctxt_a = sb("ctxt_a", [128, GB, SC])
        xn1, xn1t = sb("xn1", [128, GB, D]), sb("xn1t", [128, T])
        qb, kb = sb("qb", [128, GB, D]), sb("kb", [128, GB, D])
        qsq, ksq = sb("qsq", [128, GB, D]), sb("ksq", [128, GB, D])
        ms, rr = sb("ms", [128, 2, GB * H]), sb("rr", [128, 2, GB * H])
        nt = sb("nt", [128, 2, GB * H])
        q_st = sb("q_st", [128, GB, H, 32], F16)
        k_st = sb("k_st", [128, GB, H, 32], F16)
        q_hi, k_hi = sb("q_hi", [128, GB, D], F16), sb("k_hi", [128, GB, D], F16)
        v_st = sb("v_st", [128, GB, H, HD + 1])
        qkht = sb("qkht", [128, GB * (S + SC)], F16)
        kbd = sb("kbd", [128, GB, H, SC], F16)
        st_t = sb("st_t", [128, NQ * (S + SC)], F16)
        probs = sb("probs", [128, HQ, NQ, S])
        o_t = sb("o_t", [128, HQ * S])
        rden = sb("rden", [128, HQ, NQ])
        o_n, on_t = sb("o_n", [128, GB, D]), sb("on_t", [128, T])
        x1 = sb("x1", [128, GB, D])
        stats = sb("stats", [128, 2, GB, 6])
        mv, lnd, lnr, lnt, lnv = (sb(n, [128, 2, GB]) for n in ("mv", "lnd", "lnr", "lnt", "lnv"))

        ctxt_b, ctxn_b = sb("ctxt_b", [128, GB, SC]), sb("ctxn_b", [128, GB, D])
        xn2, xn3, xn4 = (sb(n, [128, GB, D]) for n in ("xn2", "xn3", "xn4"))
        am1, sc1, inv1 = (sb(n, [128, GB]) for n in ("am1", "sc1", "inv1"))
        xr = sb("xr", [128, GB, D])
        xi = sb("xi", [128, GB, D], BF16)
        xi_t = sb("xi_t", [128, T], BF16)
        dg = sb("dg", [128, GB, 128])
        sbc = sb("sbc", [128, GB, S])
        hs = sb("hs", [128, 2, GB, S + 2])
        cv = sb("cv", [128, 2, GB, S])
        cv1, cv2 = sb("cv1", [128, GB, S]), sb("cv2", [128, 2, GB, S])
        th = sb("th", [128, 2, GB * S])
        h2 = sb("h2", [128, KB, T])
        am2, sc2, inv2 = (sb(n, [128, GB]) for n in ("am2", "sc2", "inv2"))
        hr = sb("hr", [128, 2, HID])
        hi2 = sb("hi2", [128, 2, HID], BF16)
        hi_t = sb("hi_t", [128, GB, KB, S], BF16)
        x2, x2b = sb("x2", [128, GB, D]), sb("x2b", [128, GB, D])
        xn3t, bft = sb("xn3t", [128, T]), sb("bft", [128, T])
        nmax1 = sb("nmax1", [128, GB])
        p1, p1n = sb("p1", [128, GB, SC]), sb("p1n", [128, GB, SC])
        l1, rl1 = sb("l1", [128, GB]), sb("rl1", [128, GB])
        p1t, oct_ = sb("p1t", [128, T]), sb("oct_", [128, T])
        x3 = sb("x3", [128, GB, D])
        gmax, gsum = sb("gmax", [128, GB]), sb("gsum", [128, GB])
        gsub, gexp = sb("gsub", [128, GB, E]), sb("gexp", [128, GB, E])

        x4h, x4l = sb("x4h", [128, T], F16), sb("x4l", [128, T], F16)
        aff = sb("aff", [128, GB, E])
        tg = sb("tg", [128, 2, T])
        gw = sb("gw", [128, 2, T])
        hu = sb("hu", [128, 2, T])
        acc = sb("acc", [128, GB, D])

        pa = stack.enter_context(nc.psum_tensor("pa", [128, 4, 512], F32))
        pb = stack.enter_context(nc.psum_tensor("pb", [128, 512], F32))
        pg = stack.enter_context(nc.psum_tensor("pg", [128, 512], F32))
        pu = stack.enter_context(nc.psum_tensor("pu", [128, 512], F32))
        py = stack.enter_context(nc.psum_tensor("py", [128, GB, D], F32))
        pa16 = pa[:, 0, :].bitcast(F16)
        pb16, pbb = pb[:, :].bitcast(F16), pb[:, :].bitcast(BF16)

        small_in = signal("small_in")
        wg_in, wu_in = signal("wg_in"), signal("wu_in")
        pad_done = signal("pad_done")
        psum_clear = signal("psum_clear")
        wabs_done = signal("wabs_done")
        wsum_done = signal("wsum_done")
        setup_done = signal("setup_done")
        wg_hi, wg_used = signal("wg_hi"), signal("wg_used")
        xin_in, xres_in, ctxa_in = signal("xin_in", 16), signal("xres_in", 16), signal("ctxa_in", 16)
        xn1_done = signal("xn1_done")
        xn1t_ps, xn1t_done = signal("xn1t_ps"), signal("xn1t_done")
        q_ps, k_ps, v_ps = signal("q_ps"), signal("k_ps"), signal("v_ps")
        qb_done, kb_done = signal("qb_done"), signal("kb_done")
        qk_sq = signal("qk_sq", 2)
        v_done = signal("v_done")
        kf_done, kh_done = signal("kf_done"), signal("kh_done")
        q_hi_done, kl_done = signal("q_hi_done"), signal("kl_done")
        ql_done = signal("ql_done")
        dup_done, first_done = signal("dup_done", 2), signal("first_done", 2)
        qkht_ps, qkht_done = signal("qkht_ps"), signal("qkht_done")
        kbd_done = signal("kbd_done", GB)
        max_ps, max_done = signal("max_ps", 2 * GB), signal("max_done", 2 * GB)
        st_ps, st_done = signal("st_ps", GB), signal("st_done", GB)
        s_ps, p_done = signal("s_ps", GB), signal("p_done", GB * HQ)
        o_ps, o_done = signal("o_ps", GB), signal("o_done", GB)
        oq_ps, on_done = signal("oq_ps", GB), signal("on_done", GB)
        ont_ps, ont_done = signal("ont_ps"), signal("ont_done")
        y_ps, x1_done = signal("y_ps"), signal("x1_done")
        xres_b_done = signal("xres_b_done")
        ctxb_in = signal("ctxb_in", 32)
        xi_done, dg_done = signal("xi_done"), signal("dg_done")
        xit_ps, xit_done = signal("xit_ps"), signal("xit_done")
        sbc_ps, sbc_done = signal("sbc_ps"), signal("sbc_done")
        fc1_ps, hs_done = signal("fc1_ps", KB), signal("hs_done", KB)
        mid_done, cv_done = signal("mid_done", KB), signal("cv_done", KB)
        th_done, h2_done = signal("th_done", KB), signal("h2_done", KB)
        h2t_ps, sc2_done = signal("h2t_ps", GB), signal("sc2_done", GB)
        hr_done, hi2_done = signal("hr_done", GB), signal("hi2_done", GB)
        hit_ps, hit_done = signal("hit_ps", GB), signal("hit_done", GB)
        fc2_ps, x2_done = signal("fc2_ps"), signal("x2_done")
        x2b_done = signal("x2b_done")
        xn3_done, xn3t_ps, xn3t_done = signal("xn3_done"), signal("xn3t_ps"), signal("xn3t_done")
        bf_ps, bf_done = signal("bf_ps"), signal("bf_done")
        s1_ps, nmax1_done, p1_done = signal("s1_ps"), signal("nmax1_done"), signal("p1_done")
        p1n_done, p1t_ps, p1t_done = signal("p1n_done"), signal("p1t_ps"), signal("p1t_done")
        oc_ps, oc_done = signal("oc_ps"), signal("oc_done")
        fu_ps, xn4_done = signal("fu_ps"), signal("xn4_done")
        xn4t_ps, x4h_done, x4l_done = signal("xn4t_ps"), signal("x4h_done"), signal("x4l_done")
        lg_ps, gsub_done, gexp_done = signal("lg_ps"), signal("gsub_done"), signal("gexp_done")
        g_ps, u_ps = signal("g_ps", NU), signal("u_ps", NU)
        tg_done, gw_done, hu_done = signal("tg_done", NU), signal("gw_done", NU), signal("hu_done", NU)
        d_ps = signal("d_ps", E)
        comb_done = signal("comb_done", E)
        out_done = signal("out_done", 16)
        link_a, link_b = signal("link_a", LINKS_A), signal("link_b", LINKS_B)
        link_s = signal("link_s")

        block = stack.enter_context(nc.Block())

        def later(g):
            return not (isinstance(g, int) and g == 0)

        def periods(eng, body):
            body(0, None, None)
            body(1, 0, None)
            body(2, 1, 0)
            with eng.Fori(3, NG) as i:
                body(i, i - 1, i - 2)
            body(None, NG - 1, NG - 2)
            body(None, None, NG - 1)

        steps_a = ["xn1t", "qkv", None, None, "qkht", None]
        for t in range(GB):
            steps_a += [("max", t), ("stacks", t), ("scores", t), ("values", t), ("turn", t)]
        steps_a += ["ont", "proj"]
        steps_b = ["xit", "sbc"] + [("fc1", k) for k in range(KB)]
        for t in range(GB):
            steps_b += [("h2t", t), ("hit", t)]
        steps_b += ["fc2", "xn3t", "bf", "s1", "p1t", "oc", None, "fused", None, None]
        steps_b += [None] * (len(steps_a) - len(steps_b))
        last_b = ["xn4t", "gate"]
        parts = []
        for u in range(NU):
            parts += [("g", u), ("u", u)]
            if u:
                parts.append(("d", u - 1))
        parts.append(("d", NU - 1))
        NS = len(steps_a)

        def parts_of(s):
            return parts[s * len(parts) // NS:(s + 1) * len(parts) // NS]

        def run_slots(a, b, c, do_a, do_b, do_c):
            for s in range(NS):
                if a is not None and steps_a[s] is not None:
                    do_a(steps_a[s], a)
                if b is not None and steps_b[s] is not None:
                    do_b(steps_b[s], b)
                if c is not None:
                    for part in parts_of(s):
                        do_c(part, c)
            if b is not None:
                for step in last_b:
                    do_b(step, b)

        def split_head(ap):
            return ap.rearrange("p t (h d) -> p t h d", h=H)

        def named(step):
            return step if isinstance(step, tuple) else (step, 0)

        x_g = x.rearrange("(g t) s d -> g s t d", t=GB)
        out_g = out.rearrange("(g t) s d -> g s t d", t=GB)
        ctx_g = ctx.rearrange("(g t) s d -> g s t d", t=GB)
        ctxt_g = ctx_t.rearrange("(g t) d s -> g d t s", t=GB)

        @block.sync
        def _(sp):
            row = lambda v: v.partition_broadcast(128)
            small = [(wq_s[:, :], wq), (wk_s[:, :], wkv[:, 0:D]), (wv_s[:, :], wkv[:, D:2 * D]), (wp_s[:, :], wproj),
                     (bq_s[:, :], row(bq)), (bk_s[:, :], row(bkv[0:D])), (bv_s[:, :], row(bkv[D:2 * D])),
                     (bp_s[:, :], row(bproj)), (a2b_s[:, :], row(aw2b)), (gq_s[:, :], row(gq)), (gk_s[:, :], row(gk)),
                     (w1_f[:, :], w1t), (w2_f[:, :, :], w2t), (cw_s[:, :, :], conv_w), (cb_s[:, :], conv_b),
                     (aw1_s[:, :], aw1t), (aw1b_s[:, :], aw1b), (aw2_s[:, :, :], aw2t), (gate_f[:, :], gate),
                     (id_f[:, :], ident), (mask_f[:, :], head_mask), (wd_s[:, :, :], wd)]
            sp.dma_start(xin[:, :, :], x_g[0]).then_inc(xin_in.sem, 16)
            sp.dma_start(ctxt_a[:, :, :], ctxt_g[0]).then_inc(ctxa_in.sem, 16)
            for dst, src in small:
                sp.dma_start(dst, src).then_inc(small_in.sem, 16)
            sp.dma_start(w_stage[:, :], wg).then_inc(wg_in.sem, 16)
            sp.dma_start(xres[:, :, :], x_g[0]).then_inc(xres_in.sem, 16)
            sp.dma_start(ctxt_b[:, :, :], ctxt_g[0]).then_inc(ctxb_in.sem, 16)
            sp.dma_start(ctxn_b[0:SC, :, :], ctx_g[0]).then_inc(ctxb_in.sem, 16)
            sp.wait_ge(wg_used.sem, 1)
            sp.dma_start(w_stage[:, :], wu).then_inc(wu_in.sem, 16)

            def body(a, b, c):
                if a is not None and not (isinstance(a, int) and a == NG - 1):
                    sp.wait_ge(xn1_done.sem, xn1_done.at(a))
                    sp.dma_start(xin[:, :, :], x_g[a + 1]).then_inc(xin_in.sem, 16)
                    sp.wait_ge(v_ps.sem, v_ps.at(a))
                    sp.dma_start(ctxt_a[:, :, :], ctxt_g[a + 1]).then_inc(ctxa_in.sem, 16)
                    sp.wait_ge(xres_b_done.sem, xres_b_done.at(a))
                    sp.dma_start(xres[:, :, :], x_g[a + 1]).then_inc(xres_in.sem, 16)
                if b is not None and not (isinstance(b, int) and b == NG - 1):
                    sp.wait_ge(oc_ps.sem, oc_ps.at(b))
                    sp.dma_start(ctxt_b[:, :, :], ctxt_g[b + 1]).then_inc(ctxb_in.sem, 16)
                    sp.dma_start(ctxn_b[0:SC, :, :], ctx_g[b + 1]).then_inc(ctxb_in.sem, 16)
                if c is not None:
                    sp.wait_ge(comb_done.sem, comb_done.at(c, E))
                    sp.dma_start(out_g[c], acc[:, :, :]).then_inc(out_done.sem, 16)

            body(0, None, None)
            body(1, 0, None)
            body(2, 1, 0)
            with sp.Fori(3, NG - 1) as i:
                body(i, i - 1, i - 2)
            body(NG - 1, NG - 2, NG - 3)
            body(None, NG - 1, NG - 2)
            body(None, None, NG - 1)
            sp.wait_ge(out_done.sem, out_done.at(NG - 1, 16))

        @block.tensor
        def _(pe):
            pe.wait_ge(wabs_done.sem, 1)
            pe.matmul(pb[:, 0:2], ones[:, :], wabs[:, :], start=True, stop=True).then_inc(wsum_done.sem, 1)
            pe.wait_ge(setup_done.sem, 1)

            def do_a(step, g):
                name, t = named(step)
                if name == "xn1t":
                    pe.wait_ge(xn1_done.sem, xn1_done.at(g))
                    for j in range(GB):
                        mm = pe.transpose(pa[:, 0, j * S:(j + 1) * S], xn1[:, j, :], id_f[:, :])
                    mm.then_inc(xn1t_ps.sem, 1)
                elif name == "qkv":
                    pe.wait_ge(xn1t_done.sem, xn1t_done.at(g))
                    for j in range(GB):
                        mm = pe.matmul(pa[:, 1, j * D:(j + 1) * D], xn1t[:, j * S:(j + 1) * S], wq_s[:, :],
                                       start=True, stop=True)
                    mm.then_inc(q_ps.sem, 1)
                    pe.wait_ge(ctxa_in.sem, ctxa_in.at(g, 16))
                    for j in range(GB):
                        mm = pe.matmul(pa[0:SC, 2, j * D:(j + 1) * D], ctxt_a[:, j, :], wk_s[:, :],
                                       start=True, stop=True)
                    mm.then_inc(k_ps.sem, 1)
                    if later(g):
                        pe.wait_ge(x1_done.sem, x1_done.at(g - 1))
                    for j in range(GB):
                        mm = pe.matmul(pa[0:SC, 3, j * D:(j + 1) * D], ctxt_a[:, j, :], wv_s[:, :],
                                       start=True, stop=True)
                    mm.then_inc(v_ps.sem, 1)
                elif name == "qkht":
                    pe.wait_ge(q_hi_done.sem, q_hi_done.at(g))
                    for j in range(GB):
                        pe.transpose(pa16[:, j * S:(j + 1) * S], q_hi[:, j, :], id_h[:, :])
                    pe.wait_ge(kh_done.sem, kh_done.at(g))
                    for j in range(GB):
                        mm = pe.transpose(pa16[:, GB * S + j * SC:GB * S + (j + 1) * SC], k_hi[0:SC, j, :],
                                          id_h[0:SC, 0:SC])
                    mm.then_inc(qkht_ps.sem, 1)
                elif name == "max":
                    pe.wait_ge(kbd_done.sem, kbd_done.at(g, t + 1))
                    if t == 0:
                        pe.wait_ge(qkht_done.sem, qkht_done.at(g))
                        pe.wait_ge(v_done.sem, v_done.at(g))
                    else:
                        pe.wait_ge(on_done.sem, on_done.at(g, t))
                    for c in range(4):
                        mm = pe.matmul(pa[:, c, 0:4 * SC], qkht[:, t * S:(t + 1) * S], kbd[:, t, 4 * c:4 * c + 4, :],
                                       start=True, stop=True)
                        if c % 2:
                            mm.then_inc(max_ps.sem, 1)
                elif name == "stacks":
                    if t == 0:
                        pe.wait_ge(first_done.sem, first_done.at(g, 2))
                        pe.wait_ge(dup_done.sem, dup_done.at(g, 2))
                        pe.wait_ge(kl_done.sem, kl_done.at(g))
                    pe.wait_ge(max_done.sem, max_done.at(g, 2 * t + 2))
                    for n in range(NQ):
                        pe.transpose(pa16[:, n * S:(n + 1) * S], q_st[:, t, HQ * n:HQ * n + HQ, :], id_h[:, :])
                    for n in range(NQ):
                        mm = pe.transpose(pa16[:, NQ * S + n * SC:NQ * S + (n + 1) * SC],
                                          k_st[0:SC, t, HQ * n:HQ * n + HQ, :], id_h[0:SC, 0:SC])
                    mm.then_inc(st_ps.sem, 1)
                elif name == "scores":
                    pe.wait_ge(st_done.sem, st_done.at(g, t + 1))
                    for n in range(NQ):
                        for i in range(HQ):
                            r = slice(32 * i, 32 * i + 32)
                            mm = pe.matmul(pa[0:SC, i, n * S:(n + 1) * S],
                                           st_t[r, NQ * S + n * SC:NQ * S + (n + 1) * SC],
                                           st_t[r, n * S:(n + 1) * S], start=True, stop=True)
                    mm.then_inc(s_ps.sem, 1)
                elif name == "values":
                    for i in range(HQ):
                        pe.wait_ge(p_done.sem, p_done.at(g, HQ * t + i + 1))
                        for n in range(NQ):
                            mm = pe.matmul(pa[32 * n:32 * n + HD + 1, 0, i * S:(i + 1) * S],
                                           v_st[0:SC, t, HQ * n + i, :], probs[0:SC, i, n, :],
                                           start=True, stop=True)
                    mm.then_inc(o_ps.sem, 1)
                elif name == "turn":
                    pe.wait_ge(o_done.sem, o_done.at(g, t + 1))
                    for i in range(HQ):
                        mm = pe.transpose(pa[:, 1, i * 128:(i + 1) * 128], o_t[:, i * S:(i + 1) * S], id_f[:, :])
                    mm.then_inc(oq_ps.sem, 1)
                elif name == "ont":
                    pe.wait_ge(on_done.sem, on_done.at(g, GB))
                    for j in range(GB):
                        mm = pe.transpose(pa[:, 2, j * S:(j + 1) * S], o_n[:, j, :], id_f[:, :])
                    mm.then_inc(ont_ps.sem, 1)
                elif name == "proj":
                    pe.wait_ge(ont_done.sem, ont_done.at(g))
                    for j in range(GB):
                        mm = pe.matmul(pa[:, 3, j * D:(j + 1) * D], on_t[:, j * S:(j + 1) * S], wp_s[:, :],
                                       start=True, stop=True)
                    mm.then_inc(y_ps.sem, 1)

            def do_b(step, g):
                name, t = named(step)
                if name == "xit":
                    pe.wait_ge(xi_done.sem, xi_done.at(g))
                    if later(g):
                        pe.wait_ge(gsub_done.sem, gsub_done.at(g - 1))
                    for j in range(GB):
                        mm = pe.transpose(pbb[:, j * S:(j + 1) * S], xi[:, j, :], id_b[:, :])
                    mm.then_inc(xit_ps.sem, 1)
                elif name == "sbc":
                    pe.wait_ge(dg_done.sem, dg_done.at(g))
                    pe.wait_ge(xit_done.sem, xit_done.at(g))
                    pe.matmul(pb[:, :], ones[:, :], dg[:, :, :], start=True, stop=True).then_inc(sbc_ps.sem, 1)
                elif name == "fc1":
                    if t == 0:
                        pe.wait_ge(sbc_done.sem, sbc_done.at(g))
                    else:
                        pe.wait_ge(hs_done.sem, hs_done.at(g, t))
                    pe.matmul(pb[:, :], w1_i[:, t * 128:(t + 1) * 128], xi_t[:, :], start=True, stop=True)\
                      .then_inc(fc1_ps.sem, 1)
                elif name == "h2t":
                    if t == 0:
                        pe.wait_ge(hs_done.sem, hs_done.at(g, KB))
                        pe.wait_ge(h2_done.sem, h2_done.at(g, KB))
                    else:
                        pe.wait_ge(hit_done.sem, hit_done.at(g, t))
                    for k in range(KB):
                        mm = pe.transpose(pb[:, k * 128:(k + 1) * 128], h2[:, k, t * S:(t + 1) * S], id_f[:, :])
                    mm.then_inc(h2t_ps.sem, 1)
                elif name == "hit":
                    pe.wait_ge(hi2_done.sem, hi2_done.at(g, t + 1))
                    for k in range(KB):
                        mm = pe.transpose(pbb[:, k * S:(k + 1) * S], hi2[:, t % 2, k * 128:(k + 1) * 128], id_b[:, :])
                    mm.then_inc(hit_ps.sem, 1)
                elif name == "fc2":
                    pe.wait_ge(hit_done.sem, hit_done.at(g, GB))
                    for j in range(GB):
                        for k in range(KB):
                            mm = pe.matmul(pb[:, j * D:(j + 1) * D], hi_t[:, j, k, :], w2_i[:, k, :],
                                           start=(k == 0), stop=(k == KB - 1))
                    mm.then_inc(fc2_ps.sem, 1)
                elif name == "xn3t":
                    pe.wait_ge(xn3_done.sem, xn3_done.at(g))
                    for j in range(GB):
                        mm = pe.transpose(pb[:, j * S:(j + 1) * S], xn3[:, j, :], id_f[:, :])
                    mm.then_inc(xn3t_ps.sem, 1)
                elif name == "bf":
                    pe.wait_ge(xn3t_done.sem, xn3t_done.at(g))
                    pe.matmul(pb[:, :], aw1_s[:, :], xn3t[:, :], start=True, stop=True).then_inc(bf_ps.sem, 1)
                elif name == "s1":
                    pe.wait_ge(bf_done.sem, bf_done.at(g))
                    pe.wait_ge(ctxb_in.sem, ctxb_in.at(g, 32))
                    for j in range(GB):
                        mm = pe.matmul(pb[:, j * SC:(j + 1) * SC], bft[:, j * S:(j + 1) * S], ctxt_b[:, j, :],
                                       start=True, stop=True)
                    mm.then_inc(s1_ps.sem, 1)
                elif name == "p1t":
                    pe.wait_ge(p1n_done.sem, p1n_done.at(g))
                    for j in range(GB):
                        mm = pe.transpose(pb[0:SC, j * S:(j + 1) * S], p1n[:, j, :], id_f[:, :])
                    mm.then_inc(p1t_ps.sem, 1)
                elif name == "oc":
                    pe.wait_ge(p1t_done.sem, p1t_done.at(g))
                    for j in range(GB):
                        mm = pe.matmul(pb[:, j * S:(j + 1) * S], ctxn_b[0:SC, j, :], p1t[0:SC, j * S:(j + 1) * S],
                                       start=True, stop=True)
                    mm.then_inc(oc_ps.sem, 1)
                elif name == "fused":
                    pe.wait_ge(oc_done.sem, oc_done.at(g))
                    for j in range(GB):
                        pe.matmul(pb[:, j * D:(j + 1) * D], xn3t[:, j * S:(j + 1) * S], aw2_s[:, 0, :],
                                  start=True, stop=False)
                        mm = pe.matmul(pb[:, j * D:(j + 1) * D], oct_[:, j * S:(j + 1) * S], aw2_s[:, 1, :],
                                       start=False, stop=True)
                    mm.then_inc(fu_ps.sem, 1)
                elif name == "xn4t":
                    pe.wait_ge(xn4_done.sem, xn4_done.at(g))
                    for j in range(GB):
                        mm = pe.transpose(pb[:, j * S:(j + 1) * S], xn4[:, j, :], id_f[:, :])
                    mm.then_inc(xn4t_ps.sem, 1)
                elif name == "gate":
                    pe.wait_ge(x4l_done.sem, x4l_done.at(g))
                    for j in range(GB):
                        js = slice(j * S, (j + 1) * S)
                        o = pb[:, j * E:(j + 1) * E]
                        pe.matmul(o, x4h[:, js], gate_h[:, :], start=True, stop=False)
                        pe.matmul(o, x4h[:, js], gate_l[:, :], start=False, stop=False)
                        mm = pe.matmul(o, x4l[:, js], gate_h[:, :], start=False, stop=True)
                    mm.then_inc(lg_ps.sem, 1)

            def do_c(part, g):
                what, u = part
                us = slice(u * 128, (u + 1) * 128)
                if what in "gu":
                    if what == "g":
                        if u == 0:
                            pe.wait_ge(x4l_done.sem, x4l_done.at(g))
                            if later(g):
                                pe.wait_ge(gw_done.sem, gw_done.at(g - 1, NU))
                        else:
                            pe.wait_ge(gw_done.sem, gw_done.at(g, u))
                        o, w_hi, w_lo, done = pg, wg_h, wg_l, g_ps
                    else:
                        if u == 0:
                            if later(g):
                                pe.wait_ge(hu_done.sem, hu_done.at(g - 1, NU))
                        else:
                            pe.wait_ge(hu_done.sem, hu_done.at(g, u))
                        o, w_hi, w_lo, done = pu, wu_h, wu_l, u_ps
                    pe.matmul(o[:, :], w_hi[:, us], x4h[:, :], start=True, stop=False)
                    pe.matmul(o[:, :], w_hi[:, us], x4l[:, :], start=False, stop=False)
                    pe.matmul(o[:, :], w_lo[:, us], x4h[:, :], start=False, stop=True).then_inc(done.sem, 1)
                else:
                    e, half = divmod(u, 2)
                    if half == 0:
                        if e == 0:
                            if later(g):
                                pe.wait_ge(comb_done.sem, comb_done.at(g - 1, E))
                        else:
                            pe.wait_ge(comb_done.sem, comb_done.at(g, e))
                    pe.wait_ge(hu_done.sem, hu_done.at(g, u + 1))
                    for j in range(GB):
                        mm = pe.matmul(py[:, j, :], hu[:, u % 2, j * S:(j + 1) * S], wd_s[:, u, :],
                                       start=(half == 0 and j == 0), stop=(half == 1), skip_group_check=True)
                    if half:
                        mm.then_inc(d_ps.sem, 1)

            periods(pe, lambda a, b, c: run_slots(a, b, c, do_a, do_b, do_c))

        @block.scalar
        def _(act):
            act.wait_ge(small_in.sem, 16 * 22)
            act.activation(gate_h[:, :], gate_f[:, :], ACT.Copy, scale=WSCALE)
            act.wait_ge(wg_in.sem, 16)
            act.activation(wg_h[:, :], w_stage[:, :], ACT.Copy, scale=WSCALE).then_inc(wg_hi.sem, 1)
            act.wait_ge(wu_in.sem, 16)
            act.activation(wu_h[:, :], w_stage[:, :], ACT.Copy, scale=WSCALE).then_inc(wg_hi.sem, 1)
            act.wait_ge(pad_done.sem, 1)

            def do_a(step, g):
                name, t = named(step)
                if name == "xn1t":
                    act.wait_ge(xn1t_ps.sem, xn1t_ps.at(g))
                    act.activation(xn1t[:, :], pa[:, 0, :], ACT.Copy).then_inc(xn1t_done.sem, 1)
                elif name == "qkv":
                    act.wait_ge(qb_done.sem, qb_done.at(g))
                    act.activation(qsq[:, :, :], qb[:, :, :], ACT.Square).then_inc(qk_sq.sem, 1)
                    act.wait_ge(kb_done.sem, kb_done.at(g))
                    act.activation(ksq[0:SC, :, :], kb[0:SC, :, :], ACT.Square).then_inc(qk_sq.sem, 1)
                    act.wait_ge(kf_done.sem, kf_done.at(g))
                    act.activation(k_hi[0:SC, :, :], kb[0:SC, :, :], ACT.Copy).then_inc(kh_done.sem, 1)
                    act.wait_ge(q_hi_done.sem, q_hi_done.at(g))
                    act.activation(q_st[:, :, :, 0:HD], q_hi[:, :, :].rearrange("p t (h d) -> p t h d", h=H),
                                   ACT.Copy).then_inc(first_done.sem, 1)
                    act.wait_ge(kh_done.sem, kh_done.at(g))
                    act.activation(k_st[0:SC, :, :, 0:HD], k_hi[0:SC, :, :].rearrange("p t (h d) -> p t h d", h=H),
                                   ACT.Copy).then_inc(first_done.sem, 1)
                elif name == "qkht":
                    act.wait_ge(qkht_ps.sem, qkht_ps.at(g))
                    act.activation(qkht[:, :], pa16[:, 0:GB * (S + SC)], ACT.Copy).then_inc(qkht_done.sem, 1)
                elif name == "stacks":
                    act.wait_ge(st_ps.sem, st_ps.at(g, t + 1))
                    act.activation(st_t[:, :], pa16[:, 0:NQ * (S + SC)], ACT.Copy).then_inc(st_done.sem, 1)
                elif name == "scores":
                    act.wait_ge(s_ps.sem, s_ps.at(g, t + 1))
                    for i in range(HQ):
                        act.activation(probs[0:SC, i, :, :], pa[0:SC, i, :], ACT.Exp).then_inc(p_done.sem, 1)
                elif name == "values":
                    act.wait_ge(o_ps.sem, o_ps.at(g, t + 1))
                    act.activation(o_t[:, :], pa[:, 0, :], ACT.Copy).then_inc(o_done.sem, 1)
                elif name == "ont":
                    act.wait_ge(ont_ps.sem, ont_ps.at(g))
                    act.activation(on_t[:, :], pa[:, 2, :], ACT.Copy).then_inc(ont_done.sem, 1)

            def do_b(step, g):
                name, t = named(step)
                if name == "xit":
                    act.wait_ge(xit_ps.sem, xit_ps.at(g))
                    act.activation(xi_t[:, :], pbb[:, 0:T], ACT.Copy).then_inc(xit_done.sem, 1)
                elif name == "sbc":
                    act.wait_ge(sbc_ps.sem, sbc_ps.at(g))
                    act.activation(sbc[:, :, :], pb[:, :], ACT.Copy).then_inc(sbc_done.sem, 1)
                elif name == "fc1":
                    act.wait_ge(hs_done.sem, hs_done.at(g, t + 1))
                    act.activation(cv[:, t % 2, :, :], hs[:, t % 2, :, 1:S + 1], ACT.Identity,
                                   bias=cb_s[:, t:t + 1], scale=cw_s[:, t, 1:2]).then_inc(mid_done.sem, 1)
                    act.wait_ge(cv_done.sem, cv_done.at(g, t + 1))
                    act.activation(th[:, t % 2, :], cv2[:, t % 2, :, :], ACT.Tanh, scale=0.5).then_inc(th_done.sem, 1)
                elif name == "h2t":
                    act.wait_ge(sc2_done.sem, sc2_done.at(g, t + 1))
                    act.activation(hr[:, t % 2, :], pb[:, :], ACT.Identity, bias=magic[:, 0:1],
                                   scale=sc2[:, t:t + 1]).then_inc(hr_done.sem, 1)
                elif name == "hit":
                    act.wait_ge(hit_ps.sem, hit_ps.at(g, t + 1))
                    act.activation(hi_t[:, t, :, :], pbb[:, 0:KB * S], ACT.Copy).then_inc(hit_done.sem, 1)
                elif name == "xn3t":
                    act.wait_ge(xn3t_ps.sem, xn3t_ps.at(g))
                    act.activation(xn3t[:, :], pb[:, :], ACT.Copy).then_inc(xn3t_done.sem, 1)
                elif name == "bf":
                    act.wait_ge(bf_ps.sem, bf_ps.at(g))
                    act.activation(bft[:, :], pb[:, :], ACT.Identity, bias=aw1b_s[:, 0:1]).then_inc(bf_done.sem, 1)
                elif name == "s1":
                    act.wait_ge(nmax1_done.sem, nmax1_done.at(g))
                    for j in range(GB):
                        ins = act.activation(p1[:, j, :], pb[:, j * SC:(j + 1) * SC], ACT.Exp, bias=nmax1[:, j:j + 1],
                                             scale=D ** -0.5, accum_out=l1[:, j:j + 1])
                    ins.then_inc(p1_done.sem, 1)
                elif name == "p1t":
                    act.wait_ge(p1t_ps.sem, p1t_ps.at(g))
                    act.activation(p1t[0:SC, :], pb[0:SC, :], ACT.Copy).then_inc(p1t_done.sem, 1)
                elif name == "oc":
                    act.wait_ge(oc_ps.sem, oc_ps.at(g))
                    act.activation(oct_[:, :], pb[:, :], ACT.Copy).then_inc(oc_done.sem, 1)
                elif name == "xn4t":
                    act.wait_ge(xn4t_ps.sem, xn4t_ps.at(g))
                    act.activation(x4h[:, :], pb[:, :], ACT.Copy).then_inc(x4h_done.sem, 1)
                elif name == "gate":
                    act.wait_ge(gsub_done.sem, gsub_done.at(g))
                    act.activation(gexp[:, :, :], gsub[:, :, :], ACT.Exp, scale=1.0 / WSCALE).then_inc(gexp_done.sem, 1)

            def do_c(part, g):
                what, u = part
                if what == "g":
                    act.wait_ge(g_ps.sem, g_ps.at(g, u + 1))
                    act.activation(tg[:, u % 2, :], pg[:, :], ACT.Tanh, scale=0.5 / WSCALE).then_inc(tg_done.sem, 1)

            periods(act, lambda a, b, c: run_slots(a, b, c, do_a, do_b, do_c))

        @block.gpsimd
        def _(pool):
            for tile, value in ((ones[:, :], 1.0), (magic[:, :], MAGIC), (q_st[:, :, :, :], 0.0),
                                (ms[:, :, :], 0.0), (k_st[:, :, :, :], 0.0), (v_st[:, :, :, :], 1.0), (hs[:, :, :, :], 0.0)):
                ins = pool.memset(tile, value)
            ins.then_inc(pad_done.sem, 1)
            pool.wait_ge(pad_done.sem, 1)
            pool.memset(k_st[:, :, :, 3 * HD:3 * HD + 1], 1.0)
            pool.wait_ge(setup_done.sem, 1)

            def do_a(step, g):
                name, t = named(step)
                if name == "xn1t":
                    pool.wait_ge(xres_in.sem, xres_in.at(g, 16))
                    if later(g):
                        pool.wait_ge(x1_done.sem, x1_done.at(g - 1))
                    pool.tensor_tensor(xres_b[:, :, :], xres[:, :, :], bp_s[:, :].unsqueeze(1).broadcast_to([128, GB, D]),
                                       ALU.add).then_inc(xres_b_done.sem, 1)
                elif name == "qkv":
                    pool.wait_ge(q_hi_done.sem, q_hi_done.at(g))
                    one = ones[:, :].rearrange("p (h d) -> p h d", h=H).unsqueeze(1).broadcast_to([128, GB, H, HD])
                    pool.tensor_tensor(q_st[:, :, :, 2 * HD:3 * HD], split_head(q_hi[:, :, :]), one, ALU.mult).then_inc(dup_done.sem, 1)
                    pool.wait_ge(kh_done.sem, kh_done.at(g))
                    pool.tensor_tensor(k_st[0:SC, :, :, HD:2 * HD], split_head(k_hi[0:SC, :, :]), one[0:SC], ALU.mult).then_inc(dup_done.sem, 1)
                elif name == "qkht":
                    pool.wait_ge(qkht_done.sem, qkht_done.at(g))
                    for j in range(GB):
                        k0 = GB * S + j * SC
                        pool.tensor_tensor(kbd[:, j, :, :],
                                           qkht[:, k0:k0 + SC].unsqueeze(1).broadcast_to([128, H, SC]),
                                           mask_h[:, :].unsqueeze(2).broadcast_to([128, H, SC]), ALU.mult)\
                            .then_inc(kbd_done.sem, 1)

            def do_b(step, g):
                name, t = named(step)
                if name == "fc2":
                    pool.wait_ge(x2_done.sem, x2_done.at(g))
                    pool.tensor_tensor(x2b[:, :, :], x2[:, :, :], a2b_s[:, :].unsqueeze(1).broadcast_to([128, GB, D]),
                                       ALU.add).then_inc(x2b_done.sem, 1)

            periods(pool, lambda a, b, c: run_slots(a, b, c, do_a, do_b, lambda part, g: None))

        @block.vector
        def _(dve):
            class Chain:

                def __init__(self, sig):
                    self.sig, self.g, self.k = sig, 0, 0

                def start(self, g):
                    self.g, self.k = g, 0

                def link(self, ins):
                    self.k += 1
                    ins.then_inc(self.sig.sem, 1)
                    dve.wait_ge(self.sig.sem, self.sig.at(self.g, self.k))

                def end(self):
                    if self.k != self.sig.per:
                        raise ValueError(f"{self.k} links")

            ca, cb, cs = Chain(link_a), Chain(link_b), Chain(link_s)

            def rsqrt(chain, y, v, tmp):
                chain.link(dve.tensor_scalar(y.bitcast(I32), v.bitcast(I32), -0.5, RSQRT_SEED, ALU.mult, ALU.add))
                for _ in range(3):
                    chain.link(dve.tensor_tensor(tmp, y, y, ALU.mult))
                    chain.link(dve.scalar_tensor_tensor(out=tmp, in0=tmp, scalar=-0.5, in1=v, op0=ALU.mult, op1=ALU.mult))
                    chain.link(dve.scalar_tensor_tensor(out=y, in0=tmp, scalar=1.5, in1=y, op0=ALU.add, op1=ALU.mult))

            def layernorm(chain, n, src, dst):
                for j in range(GB):
                    ins = dve.bn_stats(stats[:, n, j, :], src[:, j, :])
                chain.link(ins)
                st, diff, ssq = stats[:, n, :, :], lnd[:, n, :], lnt[:, n, :]
                dve.tensor_tensor(diff, st[:, :, 1], st[:, :, 4], ALU.subtract)
                dve.tensor_tensor(ssq, st[:, :, 2], st[:, :, 5], ALU.add)
                chain.link(dve.tensor_tensor(mv[:, n, :], st[:, :, 1], st[:, :, 4], ALU.add))
                chain.link(dve.scalar_tensor_tensor(out=diff, in0=diff, scalar=D / 4, in1=diff,
                                                    op0=ALU.mult, op1=ALU.mult))
                chain.link(dve.tensor_tensor(ssq, ssq, diff, ALU.add))
                dve.tensor_scalar(mv[:, n, :], mv[:, n, :], 0.5, None, ALU.mult)
                chain.link(dve.tensor_scalar(lnv[:, n, :], ssq, 1.0 / D, EPS_LN, ALU.mult, ALU.add))
                rsqrt(chain, lnr[:, n, :], lnv[:, n, :], lnt[:, n, :])
                for j in range(GB):
                    ins = dve.tensor_scalar(dst[:, j, :], src[:, j, :], mv[:, n, j:j + 1], lnr[:, n, j:j + 1],
                                            ALU.subtract, ALU.mult)
                return ins

            for bank in (pa[:, :, :], pb[:, :], pg[:, :], pu[:, :], py[:, :, :]):
                dve.memset(bank, 0.0)
            dve.wait_ge(small_in.sem, 16 * 22)
            dve.wait_ge(pad_done.sem, 1)
            dve.tensor_copy(id_h[:, :], id_f[:, :])
            dve.tensor_copy(id_b[:, :], id_f[:, :])
            dve.tensor_copy(mask_h[:, :], mask_f[:, :])
            cs.link(dve.tensor_tensor(gg_s[:, :], gq_s[:, :], gk_s[:, :], ALU.mult))
            cs.link(dve.tensor_scalar(gg_s[:, :], gg_s[:, :], HD ** -0.5, None, ALU.mult))
            dve.tensor_reduce(wabs[:, 0:1], w1_f[:, :], AX.X, ALU.add, apply_absolute_value=True)
            dve.tensor_reduce(wabs[:, 1:2], w2_f[:, :, :], AX.XY, ALU.add, apply_absolute_value=True)\
               .then_inc(wabs_done.sem, 1)
            dve.wait_ge(wsum_done.sem, 1)
            cs.link(dve.tensor_scalar(wmean[:, :], pb[:, 0:2], 1.0 / (D * HID), CLIP, ALU.mult, ALU.max))
            cs.link(dve.reciprocal(winv[:, :], wmean[:, :]))
            for w, w_int, n in ((w1_f[:, :], w1_i[:, :], 0), (w2_f[:, :, :], w2_i[:, :, :], 1)):
                cs.link(dve.tensor_scalar(w, w, winv[:, n:n + 1], MAGIC, ALU.mult, ALU.add))
                cs.link(dve.tensor_scalar(w, w, MAGIC, 1.0, ALU.subtract, ALU.min))
                cs.link(dve.tensor_scalar(w_int, w, -1.0, None, ALU.max))
            for n, (w, lo, hi) in enumerate(((w_stage, wg_l, wg_h), (w_stage, wu_l, wu_h))):
                dve.wait_ge(wg_hi.sem, n + 1)
                if n == 0:
                    cs.link(dve.scalar_tensor_tensor(out=gate_l[:, :], in0=gate_f[:, :], scalar=WSCALE, in1=gate_h[:, :],
                                                     op0=ALU.mult, op1=ALU.subtract))
                ins = dve.scalar_tensor_tensor(out=lo[:, :], in0=w[:, :], scalar=WSCALE, in1=hi[:, :],
                                               op0=ALU.mult, op1=ALU.subtract)
                if n == 0:
                    ins.then_inc(wg_used.sem, 1)
            ins.then_inc(setup_done.sem, 1)
            dve.wait_ge(setup_done.sem, 1)

            def do_a(step, g):
                name, t = named(step)
                if name == "xn1t":
                    dve.wait_ge(xin_in.sem, xin_in.at(g, 16))
                    layernorm(ca, 0, xin, xn1).then_inc(xn1_done.sem, 1)
                elif name == "qkv":
                    dve.wait_ge(q_ps.sem, q_ps.at(g))
                    dve.tensor_tensor(qb[:, :, :], pa[:, 1, :].rearrange("p (t d) -> p t d", t=GB),
                                      bq_s[:, :].unsqueeze(1).broadcast_to([128, GB, D]), ALU.add)\
                       .then_inc(qb_done.sem, 1)
                    dve.wait_ge(k_ps.sem, k_ps.at(g))
                    dve.tensor_tensor(kb[0:SC, :, :], pa[0:SC, 2, :].rearrange("p (t d) -> p t d", t=GB),
                                      bk_s[0:SC, :].unsqueeze(1).broadcast_to([SC, GB, D]), ALU.add)\
                       .then_inc(kb_done.sem, 1)
                    dve.wait_ge(v_ps.sem, v_ps.at(g))
                    for j in range(GB):
                        ins = dve.tensor_tensor(v_st[0:SC, j, :, 0:HD],
                                                pa[0:SC, 3, j * D:(j + 1) * D].rearrange("p (h d) -> p h d", h=H),
                                                bv_s[0:SC, :].rearrange("p (h d) -> p h d", h=H), ALU.add)
                    ins.then_inc(v_done.sem, 1)
                    dve.wait_ge(qk_sq.sem, qk_sq.at(g, 1))
                    dve.tensor_reduce(ms[:, 0, :], qsq[:, :, :].rearrange("p t (h d) -> p (t h) d", h=H), AX.X, ALU.add)
                    dve.wait_ge(qk_sq.sem, qk_sq.at(g, 2))
                    ca.link(dve.tensor_reduce(ms[0:SC, 1, :], ksq[0:SC, :, :].rearrange("p t (h d) -> p (t h) d", h=H),
                                              AX.X, ALU.add))
                    ca.link(dve.tensor_scalar(ms[:, :, :], ms[:, :, :], 1.0 / HD, EPS_RMS, ALU.mult, ALU.add))
                    rsqrt(ca, rr[:, :, :], ms[:, :, :], nt[:, :, :])
                    rq = rr[:, 0, :].unsqueeze(2).broadcast_to([128, GB * H, HD])
                    rk = rr[0:SC, 1, :].unsqueeze(2).broadcast_to([SC, GB * H, HD])
                    q3 = qb[:, :, :].rearrange("p t (h d) -> p (t h) d", h=H)
                    k3 = kb[0:SC, :, :].rearrange("p t (h d) -> p (t h) d", h=H)
                    ca.link(dve.tensor_tensor(k3, k3, rk, ALU.mult))
                    gg = gg_s[0:SC, :].unsqueeze(1).broadcast_to([SC, GB * H, HD])
                    dve.tensor_tensor(k3, k3, gg, ALU.mult).then_inc(kf_done.sem, 1)
                    ca.link(dve.tensor_tensor(q3, q3, rq, ALU.mult))
                    q4, qh4 = split_head(qb[:, :, :]), split_head(q_hi[:, :, :])
                    dve.tensor_copy(q_hi[:, :, :], qb[:, :, :]).then_inc(q_hi_done.sem, 1)
                    dve.wait_ge(q_hi_done.sem, q_hi_done.at(g))
                    dve.tensor_tensor(q_st[:, :, :, HD:2 * HD], q4, qh4, ALU.subtract).then_inc(ql_done.sem, 1)
                    dve.wait_ge(kh_done.sem, kh_done.at(g))
                    dve.tensor_tensor(k_st[0:SC, :, :, 2 * HD:3 * HD], split_head(kb[0:SC, :, :]),
                                      split_head(k_hi[0:SC, :, :]), ALU.subtract).then_inc(kl_done.sem, 1)
                elif name == "max":
                    for c in range(2):
                        dve.wait_ge(max_ps.sem, max_ps.at(g, 2 * t + c + 1))
                        s4 = pa[:, 2 * c:2 * c + 2, 0:4 * SC].rearrange("p b (h k) -> p b h k", h=4)
                        dve.tensor_reduce(q_st[:, t, 8 * c:8 * c + 8, 3 * HD], s4, AX.X, ALU.max, negate=True)\
                           .then_inc(max_done.sem, 1)
                elif name == "turn":
                    dve.wait_ge(oq_ps.sem, oq_ps.at(g, t + 1))
                    oq = pa[:, 1, :].rearrange("p (i n d) -> p i n d", i=HQ, d=32)
                    ca.link(dve.reciprocal(rden[:, :, :], oq[:, :, :, HD]))
                    dve.tensor_tensor(o_n[:, t, :].rearrange("p (n i d) -> p i n d", n=NQ, d=HD), oq[:, :, :, 0:HD],
                                      rden[:, :, :].unsqueeze(3).broadcast_to([128, HQ, NQ, HD]), ALU.mult)\
                       .then_inc(on_done.sem, 1)
                elif name == "proj":
                    dve.wait_ge(y_ps.sem, y_ps.at(g))
                    dve.wait_ge(xres_b_done.sem, xres_b_done.at(g))
                    dve.tensor_tensor(x1[:, :, :], pa[:, 3, :].rearrange("p (t d) -> p t d", t=GB), xres_b[:, :, :],
                                      ALU.add).then_inc(x1_done.sem, 1)

            def do_b(step, g):
                name, t = named(step)
                if name == "xit":
                    dve.wait_ge(x1_done.sem, x1_done.at(g))
                    cb.link(layernorm(cb, 1, x1, xn2))
                    cb.link(dve.tensor_reduce(am1[:, :], xn2[:, :, :], AX.X, ALU.max, apply_absolute_value=True))
                    cb.link(dve.tensor_scalar(am1[:, :], am1[:, :], CLIP, None, ALU.max))
                    cb.link(dve.reciprocal(sc1[:, :], am1[:, :]))
                    cb.link(dve.tensor_scalar(sc1[:, :], sc1[:, :], 127.0, None, ALU.mult))
                    for j in range(GB):
                        ins = dve.tensor_scalar(xr[:, j, :], xn2[:, j, :], sc1[:, j:j + 1], MAGIC, ALU.mult, ALU.add)
                    cb.link(ins)
                    dve.tensor_scalar(xi[:, :, :], xr[:, :, :], MAGIC, None, ALU.subtract).then_inc(xi_done.sem, 1)
                    cb.link(dve.tensor_scalar(inv1[:, :], am1[:, :], wmean[:, 0:1], 1.0 / 127.0, ALU.mult, ALU.mult))
                    for j in range(GB):
                        ins = dve.tensor_scalar(dg[:, j, :], id_f[:, :], inv1[:, j:j + 1], None, ALU.mult)
                    ins.then_inc(dg_done.sem, 1)
                elif name == "fc1":
                    dve.wait_ge(fc1_ps.sem, fc1_ps.at(g, t + 1))
                    if t == 0:
                        dve.wait_ge(sbc_done.sem, sbc_done.at(g))
                    dve.tensor_tensor(hs[:, t % 2, :, 1:S + 1], pb[:, :].rearrange("p (t s) -> p t s", t=GB),
                                      sbc[:, :, :], ALU.mult).then_inc(hs_done.sem, 1)
                    dve.wait_ge(hs_done.sem, hs_done.at(g, t + 1))
                    dve.wait_ge(mid_done.sem, mid_done.at(g, t + 1))
                    cb.link(dve.scalar_tensor_tensor(out=cv1[:, :, :], in0=hs[:, t % 2, :, 0:S], scalar=cw_s[:, t, 0:1],
                                                     in1=cv[:, t % 2, :, :], op0=ALU.mult, op1=ALU.add))
                    dve.scalar_tensor_tensor(out=cv2[:, t % 2, :, :], in0=hs[:, t % 2, :, 2:S + 2],
                                             scalar=cw_s[:, t, 2:3], in1=cv1[:, :, :], op0=ALU.mult, op1=ALU.add)\
                       .then_inc(cv_done.sem, 1)
                    dve.wait_ge(cv_done.sem, cv_done.at(g, t + 1))
                    dve.wait_ge(th_done.sem, th_done.at(g, t + 1))
                    dve.scalar_tensor_tensor(out=h2[:, t, :], in0=th[:, t % 2, :], scalar=1.0,
                                             in1=cv2[:, t % 2, :, :].rearrange("p t s -> p (t s)"),
                                             op0=ALU.add, op1=ALU.mult).then_inc(h2_done.sem, 1)
                elif name == "h2t":
                    dve.wait_ge(h2t_ps.sem, h2t_ps.at(g, t + 1))
                    a, s = am2[:, t:t + 1], sc2[:, t:t + 1]
                    cb.link(dve.tensor_reduce(a, pb[:, :], AX.X, ALU.max, apply_absolute_value=True))
                    cb.link(dve.tensor_scalar(a, a, 0.5, CLIP, ALU.mult, ALU.max))
                    cb.link(dve.reciprocal(s, a))
                    dve.tensor_scalar(s, s, 0.5 * 127.0, None, ALU.mult).then_inc(sc2_done.sem, 1)
                    dve.wait_ge(hr_done.sem, hr_done.at(g, t + 1))
                    dve.tensor_scalar(hi2[:, t % 2, :], hr[:, t % 2, :], MAGIC, None, ALU.subtract)\
                       .then_inc(hi2_done.sem, 1)
                elif name == "fc2":
                    cb.link(dve.tensor_scalar(inv2[:, :], am2[:, :], wmean[:, 1:2], 1.0 / 127.0, ALU.mult, ALU.mult))
                    dve.wait_ge(fc2_ps.sem, fc2_ps.at(g))
                    for j in range(GB):
                        ins = dve.scalar_tensor_tensor(out=x2[:, j, :], in0=pb[:, j * D:(j + 1) * D],
                                                       scalar=inv2[:, j:j + 1], in1=x1[:, j, :],
                                                       op0=ALU.mult, op1=ALU.add)
                    ins.then_inc(x2_done.sem, 1)
                    dve.wait_ge(x2_done.sem, x2_done.at(g))
                    layernorm(cb, 1, x2, xn3).then_inc(xn3_done.sem, 1)
                elif name == "s1":
                    dve.wait_ge(s1_ps.sem, s1_ps.at(g))
                    cb.link(dve.tensor_reduce(nmax1[:, :], pb[:, 0:GB * SC].rearrange("p (t k) -> p t k", t=GB), AX.X,
                                              ALU.max, negate=True))
                    dve.tensor_scalar(nmax1[:, :], nmax1[:, :], D ** -0.5, None, ALU.mult).then_inc(nmax1_done.sem, 1)
                    dve.wait_ge(p1_done.sem, p1_done.at(g))
                    cb.link(dve.reciprocal(rl1[:, :], l1[:, :]))
                    dve.tensor_tensor(p1n[:, :, :], p1[:, :, :], rl1[:, :].unsqueeze(2).broadcast_to([128, GB, SC]),
                                      ALU.mult).then_inc(p1n_done.sem, 1)
                elif name == "fused":
                    dve.wait_ge(fu_ps.sem, fu_ps.at(g))
                    dve.wait_ge(x2b_done.sem, x2b_done.at(g))
                    cb.link(dve.tensor_tensor(x3[:, :, :], pb[:, :].rearrange("p (t d) -> p t d", t=GB), x2b[:, :, :],
                                              ALU.add))
                    layernorm(cb, 1, x3, xn4).then_inc(xn4_done.sem, 1)
                elif name == "xn4t":
                    dve.wait_ge(xn4t_ps.sem, xn4t_ps.at(g))
                    dve.wait_ge(x4h_done.sem, x4h_done.at(g))
                    dve.tensor_tensor(x4l[:, :], pb[:, :], x4h[:, :], ALU.subtract).then_inc(x4l_done.sem, 1)
                elif name == "gate":
                    dve.wait_ge(lg_ps.sem, lg_ps.at(g))
                    lg = pb[:, 0:GB * E].rearrange("p (t e) -> p t e", t=GB)
                    cb.link(dve.tensor_reduce(gmax[:, :], lg, AX.X, ALU.max))
                    dve.tensor_tensor(gsub[:, :, :], lg, gmax[:, :].unsqueeze(2).broadcast_to([128, GB, E]),
                                      ALU.subtract).then_inc(gsub_done.sem, 1)
                    dve.wait_ge(gexp_done.sem, gexp_done.at(g))
                    cb.link(dve.tensor_reduce(gsum[:, :], gexp[:, :, :], AX.X, ALU.add))
                    cb.link(dve.reciprocal(gsum[:, :], gsum[:, :]))
                    cb.link(dve.tensor_tensor(aff[:, :, :], gexp[:, :, :],
                                              gsum[:, :].unsqueeze(2).broadcast_to([128, GB, E]), ALU.mult))

            def do_c(part, g):
                what, u = part
                if what == "g":
                    dve.wait_ge(tg_done.sem, tg_done.at(g, u + 1))
                    dve.scalar_tensor_tensor(out=gw[:, u % 2, :], in0=tg[:, u % 2, :], scalar=1.0, in1=pg[:, :],
                                             op0=ALU.add, op1=ALU.mult).then_inc(gw_done.sem, 1)
                elif what == "u":
                    dve.wait_ge(u_ps.sem, u_ps.at(g, u + 1))
                    dve.wait_ge(gw_done.sem, gw_done.at(g, u + 1))
                    dve.scalar_tensor_tensor(out=hu[:, u % 2, :], in0=gw[:, u % 2, :], scalar=0.5 / WSCALE ** 2,
                                             in1=pu[:, :], op0=ALU.mult, op1=ALU.mult).then_inc(hu_done.sem, 1)
                elif u % 2:
                    e = u // 2
                    dve.wait_ge(d_ps.sem, d_ps.at(g, e + 1))
                    if e:
                        dve.wait_ge(comb_done.sem, comb_done.at(g, e))
                    else:
                        if later(g):
                            dve.wait_ge(out_done.sem, out_done.at(g - 1, 16))
                    before = acc if e else x3
                    for j in range(GB):
                        ins = dve.scalar_tensor_tensor(out=acc[:, j, :], in0=py[:, j, :], scalar=aff[:, j, e:e + 1],
                                                       in1=before[:, j, :], op0=ALU.mult, op1=ALU.add)
                    ins.then_inc(comb_done.sem, 1)

            def body(a, b, c):
                for chain, g in ((ca, a), (cb, b)):
                    if g is not None:
                        chain.start(g)
                run_slots(a, b, c, do_a, do_b, do_c)
                for chain, g in ((ca, a), (cb, b)):
                    if g is not None:
                        chain.end()

            periods(dve, body)


def kernel(x, ctx_1024, L0_xattn_Wq, L0_xattn_bq, L0_xattn_Wkv, L0_xattn_bkv, L0_xattn_Wproj, L0_xattn_bproj,
           L0_xattn_gq, L0_xattn_gk, L0_ffn_w1, L0_ffn_conv_w, L0_ffn_conv_b, L0_ffn_w2, L1_xattn_w1_w,
           L1_xattn_w1_b, L1_xattn_w2_w, L1_xattn_w2_b, L1_ffn_gate_w, L1_ffn_Wg, L1_ffn_Wu, L1_ffn_Wd):
    import numpy as np
    import concourse.bacc as bacc
    from concourse.bass_utils import run_bass_kernel_spmd

    def a(v):
        return np.asarray(v)

    arrays = {
        "x": a(x), "ctx": a(ctx_1024), "ctx_t": a(ctx_1024).transpose(0, 2, 1),
        "wq": a(L0_xattn_Wq), "bq": a(L0_xattn_bq), "wkv": a(L0_xattn_Wkv), "bkv": a(L0_xattn_bkv),
        "wproj": a(L0_xattn_Wproj), "bproj": a(L0_xattn_bproj), "gq": a(L0_xattn_gq), "gk": a(L0_xattn_gk),
        "w1t": a(L0_ffn_w1).T,
        "conv_w": a(L0_ffn_conv_w).reshape(KB, 128, 3).transpose(1, 0, 2),
        "conv_b": a(L0_ffn_conv_b).reshape(KB, 128).T,
        "w2t": a(L0_ffn_w2).T.reshape(KB, 128, D).transpose(1, 0, 2),
        "aw1t": a(L1_xattn_w1_w).T, "aw1b": a(L1_xattn_w1_b).reshape(D, 1),
        "aw2t": a(L1_xattn_w2_w).T.reshape(2, D, D).transpose(1, 0, 2), "aw2b": a(L1_xattn_w2_b),
        "gate": a(L1_ffn_gate_w),
        "wg": a(L1_ffn_Wg).transpose(1, 0, 2).reshape(D, E * I),
        "wu": a(L1_ffn_Wu).transpose(1, 0, 2).reshape(D, E * I),
        "wd": a(L1_ffn_Wd).reshape(NU, 128, D).transpose(1, 0, 2),
        "ident": np.eye(128, dtype=np.float32),
        "head_mask": np.repeat(np.eye(H, dtype=np.float32), HD, axis=0),
    }
    nc = bacc.Bacc("TRN2", target_bir_lowering=False, num_devices=1)
    arrays = {f"in_{n}": np.ascontiguousarray(v) for n, v in arrays.items()}
    args = [nc.dram_tensor(n, v.shape, mybir.dt.from_np(v.dtype), kind="ExternalInput").ap() for n, v in arrays.items()]
    result = nc.dram_tensor("out_x", (B, S, D), F32, kind="ExternalOutput").ap()
    build_program(nc, *args, result)
    r = run_bass_kernel_spmd(nc, [arrays], core_ids=[0])
    return r.results[0]["out_x"]
```

```python
from contextlib import ExitStack

import concourse.bass as bass
from concourse import mybir

F32 = mybir.dt.float32
F16 = mybir.dt.float16
BF16 = mybir.dt.bfloat16
I32 = mybir.dt.int32
ALU = mybir.AluOpType
ACT = mybir.ActivationFunctionType
AX = mybir.AxisListType

B, S, SC, D = 64, 128, 120, 128
GB = 4
NG = B // GB
T = GB * S
H = 16
HD = D // H
HQ = 4
NQ = H // HQ
HID = 512
KB = HID // 128
E, I = 8, 256
SIDE = (2, 4, 6)
NU = E * I // 128
EPS_LN, EPS_RMS, CLIP = 1e-5, 1e-6, 1e-5
MAGIC = 12582912.0
RSQRT_SEED = 1597463007.0
WSCALE = 64.0
LINKS_N, LINKS_A, LINKS_B, LINKS_D = 11, 16, 31, 27


class Signal:

    def __init__(self, sem, per):
        self.sem, self.per = sem, per

    def at(self, g, k=1):
        return g * self.per + k


TURNS = {
    "pe": ("bcacccacabcacbacbccccdacbaadbacbacaccaadaabcbaabccccddbcccacccacccbcccbaabdnbaadbaaaaacbac"
            "acbacbcaacaaaacadcababcadbcabaacabcabaadccd"),
    "act": ("ccaccbacccbbacbcaacacccddcbaaacaabaacbcadababacbcbcccacccdccbccccaacccdabdbaaabadaabaccbaa"
            "bcaacaabcacaacbcaaabacbcaaababadcbdacdccnda"),
    "dve": ("cccabcabbccccacaaacdcbccabacaaacbbacaacdbdbcbcabacacbccdcccaccccccacdbcaabaabaacabaabcaaba"
            "adnacdacabcabcaaccdaabadcbccbabaaaabacdaccd"),
    "pool": ("cbcabbdcdcbcccabcabbadccaacbadbcaaadacbbacaaaabcaacacadbbabccaacbbdcabacbacccadcccacbccadb"
            "cnccbacabbccaacaccccadaacacacaaaaadacacaabc"),
}


def build_program(nc, x, ctx, ctx_t, wq, bq, wkv, bkv, wproj, bproj, gq, gk, w1t, conv_w, conv_b,
                  w2t, aw1t, aw1b, aw2t, aw2b, gate, wg, wu, wd, ident, head_mask, out):
    stack = ExitStack()
    with stack:
        def sb(name, shape, dt=F32):
            return stack.enter_context(nc.sbuf_tensor(name, shape, dt))

        def signal(name, per=1):
            return Signal(stack.enter_context(nc.semaphore(name)), per)

        wq_s, wk_s, wv_s, wp_s = (sb(n, [128, D]) for n in ("wq_s", "wk_s", "wv_s", "wp_s"))
        bq_s, bk_s, bv_s, bp_s, a2b_s = (sb(n, [128, D]) for n in ("bq_s", "bk_s", "bv_s", "bp_s", "a2b_s"))
        gq_s, gk_s, gg_s = (sb(n, [128, HD]) for n in ("gq_s", "gk_s", "gg_s"))
        w1_i, w2_i = sb("w1_i", [128, HID], BF16), sb("w2_i", [128, KB, D], BF16)
        wabs = sb("wabs", [128, 2])
        wmean = sb("wmean", [128, 2])
        winv = sb("winv", [128, 2])
        cw_s, cb_s = sb("cw_s", [128, KB, 3]), sb("cb_s", [128, KB])
        aw1_s, aw1b_s, aw2_s = sb("aw1_s", [128, D]), sb("aw1b_s", [128, 1]), sb("aw2_s", [128, 2, D])
        gate_f = sb("gate_f", [128, E])
        gate_h, gate_l = sb("gate_h", [128, E], F16), sb("gate_l", [128, E], F16)
        wg_h, wg_l, wu_h, wu_l = (sb(n, [128, E * I], F16) for n in ("wg_h", "wg_l", "wu_h", "wu_l"))
        wd_s = sb("wd_s", [128, NU, D])
        id_f, id_h = sb("id_f", [128, 128]), sb("id_h", [128, 128], F16)
        mask_f, mask_h = sb("mask_f", [128, H]), sb("mask_h", [128, H], F16)
        ones = sb("ones", [128, 128])
        magic, unmagic = sb("magic", [128, 1]), sb("unmagic", [128, 1])

        xin, xres, xres_b = (sb(n, [128, GB, D]) for n in ("xin", "xres", "xres_b"))
        ctxt_a = sb("ctxt_a", [128, GB, SC])
        xn1, xn1t = sb("xn1", [128, GB, D]), sb("xn1t", [128, T])
        qb, kb = sb("qb", [128, GB, D]), sb("kb", [128, GB, D])
        qsq, ksq = sb("qsq", [128, GB, D]), sb("ksq", [128, GB, D])
        ms, rr = sb("ms", [128, 2, GB * H]), sb("rr", [128, 2, GB * H])
        root = sb("root", [128, 2, GB * H])
        nt = sb("nt", [128, 2, GB * H])
        q_st = sb("q_st", [128, GB, H, 32], F16)
        k_st = sb("k_st", [128, GB, H, 32], F16)
        q_hi, k_hi = sb("q_hi", [128, GB, D], F16), sb("k_hi", [128, GB, D], F16)
        v_st = sb("v_st", [128, GB, H, HD + 1])
        qkht = sb("qkht", [128, GB * (S + SC)], F16)
        kbd = sb("kbd", [128, GB, H, SC], F16)
        w_stage = kbd[:, :, :, :].rearrange("p t h k -> p (t h k)")[:, 0:2 * E * I].bitcast(F32)
        st_t = sb("st_t", [128, NQ * (S + SC)], F16)
        probs = sb("probs", [128, HQ, NQ, S])
        w1_f, w2_f = probs[:, 0, :, :].rearrange("p n s -> p (n s)"), probs[:, 1, :, :]
        o_t = sb("o_t", [128, HQ * S])
        rden = sb("rden", [128, HQ, NQ])
        o_n, on_t = sb("o_n", [128, GB, D]), sb("on_t", [128, T])
        x1 = sb("x1", [128, GB, D])
        stats = sb("stats", [128, 3, GB, 6])
        mv = sb("mv", [128, 3, GB, 2])
        lnd, lnr, lnt, lnv, lnm = (sb(n, [128, 3, GB]) for n in ("lnd", "lnr", "lnt", "lnv", "lnm"))

        ctxt_b, ctxn_b = sb("ctxt_b", [128, GB, SC]), sb("ctxn_b", [128, GB, D])
        xn2, xn3, xn4 = (sb(n, [128, GB, D]) for n in ("xn2", "xn3", "xn4"))
        am1, sc1, inv1 = (sb(n, [128, GB]) for n in ("am1", "sc1", "inv1"))
        xr = sb("xr", [128, GB, D])
        xi_t = sb("xi_t", [128, T], BF16)
        dg = sb("dg", [128, GB, 128])
        sbc = sb("sbc", [128, GB, S])
        hs = sb("hs", [128, 2, GB, S + 2])
        cv = sb("cv", [128, 2, GB, S])
        cv1, cv2 = sb("cv1", [128, GB, S]), sb("cv2", [128, 2, GB, S])
        th = sb("th", [128, 2, GB * S])
        h2 = sb("h2", [128, KB, T])
        am2, sc2, inv2 = (sb(n, [128, GB]) for n in ("am2", "sc2", "inv2"))
        hr = sb("hr", [128, 2, HID])
        hi_t = sb("hi_t", [128, GB, KB, S], BF16)
        x2, x2b = sb("x2", [128, GB, D]), sb("x2b", [128, GB, D])
        xn3t, bft = sb("xn3t", [128, T]), sb("bft", [128, T])
        nmax1 = sb("nmax1", [128, GB])
        p1, p1n = sb("p1", [128, GB, SC]), sb("p1n", [128, GB, SC])
        l1, rl1 = sb("l1", [128, GB]), sb("rl1", [128, GB])
        p1t, oct_ = sb("p1t", [128, T]), sb("oct_", [128, T])
        x3 = sb("x3", [128, GB, D])
        gmax, gsum = sb("gmax", [128, GB]), sb("gsum", [128, GB])
        gsub, gexp = sb("gsub", [128, GB, E]), sb("gexp", [128, GB, E])

        x4h, x4l = sb("x4h", [128, T], F16), sb("x4l", [128, T], F16)
        aff = sb("aff", [128, GB, E])
        tg = sb("tg", [128, 2, T])
        gw, us, hu = (sb(n, [128, 3, T]) for n in ("gw", "us", "hu"))
        acc, acc2 = sb("acc", [128, GB, D]), sb("acc2", [128, GB, D])
        side = sb("side", [128, 2, GB, D])

        pa = stack.enter_context(nc.psum_tensor("pa", [128, 4, 512], F32))
        pb = stack.enter_context(nc.psum_tensor("pb", [128, 512], F32))
        pg = stack.enter_context(nc.psum_tensor("pg", [128, 512], F32))
        pu = stack.enter_context(nc.psum_tensor("pu", [128, 512], F32))
        py = stack.enter_context(nc.psum_tensor("py", [128, GB, D], F32))
        BM, BO = 2, 3
        pa16, pm16 = pa[:, 0, :].bitcast(F16), pa[:, BM, :].bitcast(F16)

        small_in = signal("small_in")
        wg_in, wu_in = signal("wg_in"), signal("wu_in")
        pad_done = signal("pad_done")
        psum_clear = signal("psum_clear")
        wabs_done = signal("wabs_done")
        wsum_done = signal("wsum_done")
        setup_done = signal("setup_done")
        wg_hi, wg_used = signal("wg_hi"), signal("wg_used")
        xin_in, xres_in, ctxa_in = signal("xin_in", 16), signal("xres_in", 16), signal("ctxa_in", 16)
        ln1_ready, xn1_done = signal("ln1_ready"), signal("xn1_done")
        xn1t_ps, xn1t_done = signal("xn1t_ps"), signal("xn1t_done")
        q_ps, k_ps, v_ps = signal("q_ps"), signal("k_ps"), signal("v_ps")
        qb_done, kb_done = signal("qb_done"), signal("kb_done")
        qk_sq = signal("qk_sq", 2)
        v_done = signal("v_done")
        kf_done, kh_done = signal("kf_done"), signal("kh_done")
        q_hi_done, kl_done = signal("q_hi_done"), signal("kl_done")
        ql_done = signal("ql_done")
        dup_done, first_done = signal("dup_done", 2), signal("first_done", 2)
        qkht_ps, qkht_done = signal("qkht_ps"), signal("qkht_done")
        kbd_done = signal("kbd_done", GB)
        max_ps, max_done = signal("max_ps", 4 * GB), signal("max_done", 4 * GB)
        st_ps, st_done = signal("st_ps", GB), signal("st_done", GB)
        s_ps, p_done = signal("s_ps", 2 * GB), signal("p_done", GB * HQ)
        o_ps, o_done = signal("o_ps", GB), signal("o_done", GB)
        oq_ps, on_done = signal("oq_ps", GB), signal("on_done", GB)
        ont_ps, ont_done = signal("ont_ps"), signal("ont_done")
        y_ps, x1_done = signal("y_ps"), signal("x1_done")
        xres_b_done = signal("xres_b_done")
        ctxb_in = signal("ctxb_in", 32)
        ln2_ready, xn2_done, sc1_done = signal("ln2_ready"), signal("xn2_done"), signal("sc1_done")
        xr_done, dg_done = signal("xr_done"), signal("dg_done")
        xit_ps, xit_done = signal("xit_ps"), signal("xit_done")
        sbc_ps, sbc_done = signal("sbc_ps"), signal("sbc_done")
        fc1_ps, hs_done = signal("fc1_ps", KB), signal("hs_done", KB)
        mid_done, cv_done = signal("mid_done", KB), signal("cv_done", KB)
        th_done, h2_done = signal("th_done", KB), signal("h2_done", KB)
        h2t_ps, sc2_done = signal("h2t_ps", GB), signal("sc2_done", GB)
        hr_done = signal("hr_done", GB)
        hit_ps, hit_done = signal("hit_ps", GB), signal("hit_done", GB)
        fc2_ps, x2_done = signal("fc2_ps"), signal("x2_done")
        x2b_done = signal("x2b_done")
        ln_ready = signal("ln_ready", 2)
        xn3_done, xn3t_ps, xn3t_done = signal("xn3_done"), signal("xn3t_ps"), signal("xn3t_done")
        bf_ps, bf_done = signal("bf_ps"), signal("bf_done")
        s1_ps, nmax1_done, p1_done = signal("s1_ps"), signal("nmax1_done"), signal("p1_done")
        p1n_done, p1t_ps, p1t_done = signal("p1n_done"), signal("p1t_ps"), signal("p1t_done")
        oc_ps, oc_done = signal("oc_ps"), signal("oc_done")
        x3_done = signal("x3_done")
        fu_ps, xn4_done = signal("fu_ps"), signal("xn4_done")
        xn4t_ps, x4h_done, x4l_done = signal("xn4t_ps"), signal("x4h_done"), signal("x4l_done")
        lg_ps, gsub_done, gexp_done = signal("lg_ps"), signal("gsub_done"), signal("gexp_done")
        g_ps, u_ps = signal("g_ps", NU), signal("u_ps", NU)
        tg_done, gw_done, hu_done = signal("tg_done", NU), signal("gw_done", NU), signal("hu_done", NU)
        us_done = signal("us_done", NU)
        d_ps = signal("d_ps", E)
        comb_done, side_done = signal("comb_done", E - len(SIDE)), signal("side_done", len(SIDE))
        sum_done = signal("sum_done", len(SIDE))
        aff_done = signal("aff_done")
        out_done = signal("out_done", 16)
        link_n, link_a = signal("link_n", LINKS_N), signal("link_a", LINKS_A)
        link_b, link_d = signal("link_b", LINKS_B), signal("link_d", LINKS_D)
        link_s = signal("link_s")

        block = stack.enter_context(nc.Block())

        def later(g):
            return not (isinstance(g, int) and g == 0)

        def periods(eng, body):
            body(0, None, None, None, None)
            body(1, 0, None, None, None)
            body(2, 1, 0, None, None)
            body(3, 2, 1, 0, None)
            body(4, 3, 2, 1, 0)
            with eng.Fori(5, NG) as i:
                body(i, i - 1, i - 2, i - 3, i - 4)
            body(None, NG - 1, NG - 2, NG - 3, NG - 4)
            body(None, None, NG - 1, NG - 2, NG - 3)
            body(None, None, None, NG - 1, NG - 2)
            body(None, None, None, None, NG - 1)

        a_steps = ["xn1t", "qkv", "rms", "rms_k", "rms_q", "qkht"] + [("max", 0, c) for c in range(4)]
        a_steps.append(("stacks", 0))
        for t in range(GB):
            steps = [("scores", t, 0), ("max", t + 1, 0), ("scores", t, 1), ("values", t, 0), ("max", t + 1, 1),
                     ("values", t, 1), ("max", t + 1, 2), ("max", t + 1, 3), ("turn", t), ("stacks", t + 1)]
            a_steps += [step for step in steps if not (step[0] in ("max", "stacks") and step[1] == GB)]
        a_steps += ["ont", "proj"]
        b_steps = ["ln2", "quant", "xit", "sbc"]
        for k in range(KB + 1):
            steps = [("taps", k - 1), ("fc1", k), ("silu", k - 1)]
            b_steps += [step for step in steps if 0 <= step[1] < KB]
        b_steps += [(name, t) for t in range(GB) for name in ("h2t", "hit")] + ["fc2"]
        d_steps = ["ln3", "xn3t", "bf", "s1", "p1n", "p1t", "oc", "fused", "ln4", "xn4t", "gate"]
        c_steps = []
        for u in range(NU):
            c_steps += [("g", u), ("u", u)] + ([("d", u - 2)] if u >= 2 else [])
        c_steps += [("d", NU - 2), ("d", NU - 1)]
        stage_steps = {"n": ["ln1"], "a": a_steps, "b": b_steps, "d": d_steps, "c": c_steps}

        def run_turns(engine, n, a, b, d, c, do_a, do_b, do_c):
            groups = {"n": n, "a": a, "b": b, "d": d, "c": c}
            do = {"n": do_a, "a": do_a, "b": do_b, "d": do_b, "c": do_c}
            steps = {stage: iter(stage_steps[stage]) for stage in groups}
            for stage in TURNS[engine]:
                step = next(steps[stage])
                if groups[stage] is not None:
                    do[stage](step, groups[stage])

        def split_head(ap):
            return ap.rearrange("p t (h d) -> p t h d", h=H)

        def nth(e):
            return sum(1 for other in range(e + 1) if (other in SIDE) == (e in SIDE))

        def named(step):
            return (step, 0, 0) if isinstance(step, str) else (*step, 0)[:3]

        x_g = x.rearrange("(g t) s d -> g s t d", t=GB)
        out_g = out.rearrange("(g t) s d -> g s t d", t=GB)
        ctx_g = ctx.rearrange("(g t) s d -> g s t d", t=GB)
        ctxt_g = ctx_t.rearrange("(g t) d s -> g d t s", t=GB)

        @block.sync
        def _(sp):
            row = lambda v: v.partition_broadcast(128)
            small = [(wq_s[:, :], wq), (wk_s[:, :], wkv[:, 0:D]), (wv_s[:, :], wkv[:, D:2 * D]), (wp_s[:, :], wproj),
                     (bq_s[:, :], row(bq)), (bk_s[:, :], row(bkv[0:D])), (bv_s[:, :], row(bkv[D:2 * D])),
                     (bp_s[:, :], row(bproj)), (a2b_s[:, :], row(aw2b)), (gq_s[:, :], row(gq)), (gk_s[:, :], row(gk)),
                     (w1_f, w1t), (w2_f, w2t), (cw_s[:, :, :], conv_w), (cb_s[:, :], conv_b),
                     (aw1_s[:, :], aw1t), (aw1b_s[:, :], aw1b), (aw2_s[:, :, :], aw2t), (gate_f[:, :], gate),
                     (id_f[:, :], ident), (mask_f[:, :], head_mask), (wd_s[:, :, :], wd)]
            sp.dma_start(xin[:, :, :], x_g[0]).then_inc(xin_in.sem, 16)
            sp.dma_start(ctxt_a[:, :, :], ctxt_g[0]).then_inc(ctxa_in.sem, 16)
            for dst, src in small:
                sp.dma_start(dst, src).then_inc(small_in.sem, 16)
            sp.dma_start(w_stage, wg).then_inc(wg_in.sem, 16)
            sp.dma_start(xres[:, :, :], x_g[0]).then_inc(xres_in.sem, 16)
            sp.dma_start(ctxt_b[:, :, :], ctxt_g[0]).then_inc(ctxb_in.sem, 16)
            sp.dma_start(ctxn_b[0:SC, :, :], ctx_g[0]).then_inc(ctxb_in.sem, 16)
            sp.wait_ge(wg_used.sem, 1)
            sp.dma_start(w_stage, wu).then_inc(wu_in.sem, 16)

            def body(n, a, b, d, c):
                if n is not None and not (isinstance(n, int) and n == NG - 1):
                    sp.wait_ge(xn1_done.sem, xn1_done.at(n))
                    sp.dma_start(xin[:, :, :], x_g[n + 1]).then_inc(xin_in.sem, 16)
                if a is not None and not (isinstance(a, int) and a == NG - 1):
                    sp.wait_ge(v_ps.sem, v_ps.at(a))
                    sp.dma_start(ctxt_a[:, :, :], ctxt_g[a + 1]).then_inc(ctxa_in.sem, 16)
                    sp.wait_ge(xres_b_done.sem, xres_b_done.at(a))
                    sp.dma_start(xres[:, :, :], x_g[a + 1]).then_inc(xres_in.sem, 16)
                if d is not None and not (isinstance(d, int) and d == NG - 1):
                    sp.wait_ge(oc_ps.sem, oc_ps.at(d))
                    sp.dma_start(ctxt_b[:, :, :], ctxt_g[d + 1]).then_inc(ctxb_in.sem, 16)
                    sp.dma_start(ctxn_b[0:SC, :, :], ctx_g[d + 1]).then_inc(ctxb_in.sem, 16)
                if c is not None:
                    sp.wait_ge(sum_done.sem, sum_done.at(c, len(SIDE)))
                    sp.dma_start(out_g[c], acc2[:, :, :]).then_inc(out_done.sem, 16)

            body(0, None, None, None, None)
            body(1, 0, None, None, None)
            body(2, 1, 0, None, None)
            body(3, 2, 1, 0, None)
            body(4, 3, 2, 1, 0)
            with sp.Fori(5, NG - 1) as i:
                body(i, i - 1, i - 2, i - 3, i - 4)
            body(NG - 1, NG - 2, NG - 3, NG - 4, NG - 5)
            body(None, NG - 1, NG - 2, NG - 3, NG - 4)
            body(None, None, NG - 1, NG - 2, NG - 3)
            body(None, None, None, NG - 1, NG - 2)
            body(None, None, None, None, NG - 1)
            sp.wait_ge(out_done.sem, out_done.at(NG - 1, 16))

        @block.tensor
        def _(pe):
            pe.wait_ge(wabs_done.sem, 1)
            pe.matmul(pb[:, 0:2], ones[:, :], wabs[:, :], start=True, stop=True).then_inc(wsum_done.sem, 1)
            pe.wait_ge(setup_done.sem, 1)

            def do_a(step, g):
                name, t, c = named(step)
                if name == "xn1t":
                    pe.wait_ge(xn1_done.sem, xn1_done.at(g))
                    for j in range(GB):
                        mm = pe.transpose(pa[:, 0, j * S:(j + 1) * S], xn1[:, j, :], id_f[:, :])
                    mm.then_inc(xn1t_ps.sem, 1)
                elif name == "qkv":
                    pe.wait_ge(xn1t_done.sem, xn1t_done.at(g))
                    for j in range(GB):
                        mm = pe.matmul(pa[:, 1, j * D:(j + 1) * D], xn1t[:, j * S:(j + 1) * S], wq_s[:, :],
                                       start=True, stop=True)
                    mm.then_inc(q_ps.sem, 1)
                    pe.wait_ge(ctxa_in.sem, ctxa_in.at(g, 16))
                    for j in range(GB):
                        mm = pe.matmul(pa[0:SC, 2, j * D:(j + 1) * D], ctxt_a[:, j, :], wk_s[:, :],
                                       start=True, stop=True)
                    mm.then_inc(k_ps.sem, 1)
                    if later(g):
                        pe.wait_ge(x1_done.sem, x1_done.at(g - 1))
                    for j in range(GB):
                        mm = pe.matmul(pa[0:SC, 3, j * D:(j + 1) * D], ctxt_a[:, j, :], wv_s[:, :],
                                       start=True, stop=True)
                    mm.then_inc(v_ps.sem, 1)
                elif name == "qkht":
                    pe.wait_ge(q_hi_done.sem, q_hi_done.at(g))
                    for j in range(GB):
                        pe.transpose(pa16[:, j * S:(j + 1) * S], q_hi[:, j, :], id_h[:, :])
                    pe.wait_ge(kh_done.sem, kh_done.at(g))
                    for j in range(GB):
                        mm = pe.transpose(pa16[:, GB * S + j * SC:GB * S + (j + 1) * SC], k_hi[0:SC, j, :],
                                          id_h[0:SC, 0:SC])
                    mm.then_inc(qkht_ps.sem, 1)
                elif name == "max":
                    if c == 0:
                        pe.wait_ge(kbd_done.sem, kbd_done.at(g, t + 1))
                        if t == 0:
                            pe.wait_ge(qkht_done.sem, qkht_done.at(g))
                    else:
                        pe.wait_ge(max_done.sem, max_done.at(g, 4 * t + c))
                    pe.matmul(pa[:, BM, 0:4 * SC], qkht[:, t * S:(t + 1) * S], kbd[:, t, 4 * c:4 * c + 4, :],
                              start=True, stop=True).then_inc(max_ps.sem, 1)
                elif name == "stacks":
                    if t == 0:
                        pe.wait_ge(first_done.sem, first_done.at(g, 2))
                        pe.wait_ge(dup_done.sem, dup_done.at(g, 2))
                        pe.wait_ge(ql_done.sem, ql_done.at(g))
                        pe.wait_ge(kl_done.sem, kl_done.at(g))
                    pe.wait_ge(max_done.sem, max_done.at(g, 4 * t + 4))
                    for n in range(NQ):
                        pe.transpose(pm16[:, n * S:(n + 1) * S], q_st[:, t, HQ * n:HQ * n + HQ, :], id_h[:, :])
                    for n in range(NQ):
                        mm = pe.transpose(pm16[:, NQ * S + n * SC:NQ * S + (n + 1) * SC],
                                          k_st[0:SC, t, HQ * n:HQ * n + HQ, :], id_h[0:SC, 0:SC])
                    mm.then_inc(st_ps.sem, 1)
                elif name == "scores":
                    if c == 0:
                        pe.wait_ge(st_done.sem, st_done.at(g, t + 1))
                    else:
                        pe.wait_ge(p_done.sem, p_done.at(g, 4 * t + 2))
                    for n in range(NQ):
                        for i in (2 * c, 2 * c + 1):
                            r = slice(32 * i, 32 * i + 32)
                            mm = pe.matmul(pa[0:SC, i % 2, n * S:(n + 1) * S],
                                           st_t[r, NQ * S + n * SC:NQ * S + (n + 1) * SC],
                                           st_t[r, n * S:(n + 1) * S], start=True, stop=True)
                    mm.then_inc(s_ps.sem, 1)
                elif name == "values":
                    if c == 0:
                        if t == 0:
                            pe.wait_ge(v_done.sem, v_done.at(g))
                        else:
                            pe.wait_ge(on_done.sem, on_done.at(g, t))
                    for i in (2 * c, 2 * c + 1):
                        pe.wait_ge(p_done.sem, p_done.at(g, 4 * t + i + 1))
                        for n in range(NQ):
                            mm = pe.matmul(pa[32 * n:32 * n + HD + 1, BO, i * S:(i + 1) * S],
                                           v_st[0:SC, t, HQ * n + i, :], probs[0:SC, i, n, :],
                                           start=True, stop=True)
                    if c == 1:
                        mm.then_inc(o_ps.sem, 1)
                elif name == "turn":
                    pe.wait_ge(o_done.sem, o_done.at(g, t + 1))
                    for i in range(HQ):
                        mm = pe.transpose(pa[:, BO, i * 128:(i + 1) * 128], o_t[:, i * S:(i + 1) * S], id_f[:, :])
                    mm.then_inc(oq_ps.sem, 1)
                elif name == "ont":
                    pe.wait_ge(on_done.sem, on_done.at(g, GB))
                    for j in range(GB):
                        mm = pe.transpose(pa[:, BM, j * S:(j + 1) * S], o_n[:, j, :], id_f[:, :])
                    mm.then_inc(ont_ps.sem, 1)
                elif name == "proj":
                    pe.wait_ge(ont_done.sem, ont_done.at(g))
                    for j in range(GB):
                        mm = pe.matmul(pa[:, BO, j * D:(j + 1) * D], on_t[:, j * S:(j + 1) * S], wp_s[:, :],
                                       start=True, stop=True)
                    mm.then_inc(y_ps.sem, 1)

            pb_read = {"xit": (xit_done, 1), "sbc": (sbc_done, 1), "fc2": (x2_done, 1), "xn3t": (xn3t_done, 1),
                       "bf": (bf_done, 1), "s1": (p1_done, 1), "p1t": (p1t_done, 1), "oc": (oc_done, 1),
                       "fused": (x3_done, 1), "xn4t": (x4l_done, 1), "gate": (gsub_done, 1)}
            pb_read.update({("fc1", k): (hs_done, k + 1) for k in range(KB)})
            pb_read.update({("h2t", t): (hr_done, t + 1) for t in range(GB)})
            pb_read.update({("hit", t): (hit_done, t + 1) for t in range(GB)})
            pb_last = []

            def do_b(step, g):
                name, t, c = named(step)
                if step in pb_read:
                    if name == "hit":
                        pe.wait_ge(hr_done.sem, hr_done.at(g, t + 1))
                    if pb_last:
                        before, group = pb_last.pop()
                        read, k = pb_read[before]
                        pe.wait_ge(read.sem, read.at(group, k))
                    pb_last.append((step, g))
                if name == "xit":
                    pe.wait_ge(xr_done.sem, xr_done.at(g))
                    for j in range(GB):
                        mm = pe.transpose(pb[:, j * S:(j + 1) * S], xr[:, j, :], id_f[:, :])
                    mm.then_inc(xit_ps.sem, 1)
                elif name == "sbc":
                    pe.wait_ge(dg_done.sem, dg_done.at(g))
                    pe.matmul(pb[:, :], ones[:, :], dg[:, :, :], start=True, stop=True).then_inc(sbc_ps.sem, 1)
                elif name == "fc1":
                    if t == 0:
                        pe.wait_ge(xit_done.sem, xit_done.at(g))
                    pe.matmul(pb[:, :], w1_i[:, t * 128:(t + 1) * 128], xi_t[:, :], start=True, stop=True)\
                      .then_inc(fc1_ps.sem, 1)
                elif name == "h2t":
                    if t == 0:
                        pe.wait_ge(h2_done.sem, h2_done.at(g, KB))
                    for k in range(KB):
                        mm = pe.transpose(pb[:, k * 128:(k + 1) * 128], h2[:, k, t * S:(t + 1) * S], id_f[:, :])
                    mm.then_inc(h2t_ps.sem, 1)
                elif name == "hit":
                    for k in range(KB):
                        mm = pe.transpose(pb[:, k * S:(k + 1) * S], hr[:, t % 2, k * 128:(k + 1) * 128], id_f[:, :])
                    mm.then_inc(hit_ps.sem, 1)
                elif name == "fc2":
                    pe.wait_ge(hit_done.sem, hit_done.at(g, GB))
                    for j in range(GB):
                        for k in range(KB):
                            mm = pe.matmul(pb[:, j * D:(j + 1) * D], hi_t[:, j, k, :], w2_i[:, k, :],
                                           start=(k == 0), stop=(k == KB - 1))
                    mm.then_inc(fc2_ps.sem, 1)
                elif name == "xn3t":
                    pe.wait_ge(xn3_done.sem, xn3_done.at(g))
                    for j in range(GB):
                        mm = pe.transpose(pb[:, j * S:(j + 1) * S], xn3[:, j, :], id_f[:, :])
                    mm.then_inc(xn3t_ps.sem, 1)
                elif name == "bf":
                    pe.wait_ge(xn3t_done.sem, xn3t_done.at(g))
                    pe.matmul(pb[:, :], aw1_s[:, :], xn3t[:, :], start=True, stop=True).then_inc(bf_ps.sem, 1)
                elif name == "s1":
                    pe.wait_ge(bf_done.sem, bf_done.at(g))
                    pe.wait_ge(ctxb_in.sem, ctxb_in.at(g, 32))
                    for j in range(GB):
                        mm = pe.matmul(pb[:, j * SC:(j + 1) * SC], bft[:, j * S:(j + 1) * S], ctxt_b[:, j, :],
                                       start=True, stop=True)
                    mm.then_inc(s1_ps.sem, 1)
                elif name == "p1t":
                    pe.wait_ge(p1n_done.sem, p1n_done.at(g))
                    for j in range(GB):
                        mm = pe.transpose(pb[0:SC, j * S:(j + 1) * S], p1n[:, j, :], id_f[:, :])
                    mm.then_inc(p1t_ps.sem, 1)
                elif name == "oc":
                    pe.wait_ge(p1t_done.sem, p1t_done.at(g))
                    for j in range(GB):
                        mm = pe.matmul(pb[:, j * S:(j + 1) * S], ctxn_b[0:SC, j, :], p1t[0:SC, j * S:(j + 1) * S],
                                       start=True, stop=True)
                    mm.then_inc(oc_ps.sem, 1)
                elif name == "fused":
                    pe.wait_ge(oc_done.sem, oc_done.at(g))
                    for j in range(GB):
                        pe.matmul(pb[:, j * D:(j + 1) * D], xn3t[:, j * S:(j + 1) * S], aw2_s[:, 0, :],
                                  start=True, stop=False)
                        mm = pe.matmul(pb[:, j * D:(j + 1) * D], oct_[:, j * S:(j + 1) * S], aw2_s[:, 1, :],
                                       start=False, stop=True)
                    mm.then_inc(fu_ps.sem, 1)
                elif name == "xn4t":
                    pe.wait_ge(xn4_done.sem, xn4_done.at(g))
                    for j in range(GB):
                        mm = pe.transpose(pb[:, j * S:(j + 1) * S], xn4[:, j, :], id_f[:, :])
                    mm.then_inc(xn4t_ps.sem, 1)
                elif name == "gate":
                    pe.wait_ge(x4l_done.sem, x4l_done.at(g))
                    for j in range(GB):
                        js = slice(j * S, (j + 1) * S)
                        o = pb[:, j * E:(j + 1) * E]
                        pe.matmul(o, x4h[:, js], gate_h[:, :], start=True, stop=False)
                        pe.matmul(o, x4h[:, js], gate_l[:, :], start=False, stop=False)
                        mm = pe.matmul(o, x4l[:, js], gate_h[:, :], start=False, stop=True)
                    mm.then_inc(lg_ps.sem, 1)

            def do_c(part, g):
                what, u = part
                us = slice(u * 128, (u + 1) * 128)
                if what in "gu":
                    if what == "g":
                        if u == 0:
                            pe.wait_ge(x4l_done.sem, x4l_done.at(g))
                            if later(g):
                                pe.wait_ge(gw_done.sem, gw_done.at(g - 1, NU))
                        else:
                            pe.wait_ge(gw_done.sem, gw_done.at(g, u))
                        o, w_hi, w_lo, done = pg, wg_h, wg_l, g_ps
                    else:
                        if u == 0:
                            if later(g):
                                pe.wait_ge(us_done.sem, us_done.at(g - 1, NU))
                        else:
                            pe.wait_ge(us_done.sem, us_done.at(g, u))
                        o, w_hi, w_lo, done = pu, wu_h, wu_l, u_ps
                    pe.matmul(o[:, :], w_hi[:, us], x4h[:, :], start=True, stop=False)
                    pe.matmul(o[:, :], w_hi[:, us], x4l[:, :], start=False, stop=False)
                    pe.matmul(o[:, :], w_lo[:, us], x4h[:, :], start=False, stop=True).then_inc(done.sem, 1)
                else:
                    e, half = divmod(u, 2)
                    if half == 0:
                        if e == 0:
                            if later(g):
                                pe.wait_ge(comb_done.sem, comb_done.at(g - 1, nth(E - 1)))
                        elif e - 1 in SIDE:
                            pe.wait_ge(side_done.sem, side_done.at(g, nth(e - 1)))
                        else:
                            pe.wait_ge(comb_done.sem, comb_done.at(g, nth(e - 1)))
                    pe.wait_ge(hu_done.sem, hu_done.at(g, u + 1))
                    for j in range(GB):
                        mm = pe.matmul(py[:, j, :], hu[:, u % 3, j * S:(j + 1) * S], wd_s[:, u, :],
                                       start=(half == 0 and j == 0), stop=(half == 1), skip_group_check=True)
                    if half:
                        mm.then_inc(d_ps.sem, 1)

            def body(n, a, b, d, c):
                if pb_last:
                    step, _ = pb_last.pop()
                    pb_last.append((step, c if step in d_steps else d))
                run_turns("pe", n, a, b, d, c, do_a, do_b, do_c)

            periods(pe, body)

        @block.scalar
        def _(act):
            act.wait_ge(small_in.sem, 16 * 22)
            act.activation(gate_h[:, :], gate_f[:, :], ACT.Copy, scale=WSCALE)
            act.wait_ge(wg_in.sem, 16)
            act.activation(wg_h[:, :], w_stage, ACT.Copy, scale=WSCALE).then_inc(wg_hi.sem, 1)
            act.wait_ge(wu_in.sem, 16)
            act.activation(wu_h[:, :], w_stage, ACT.Copy, scale=WSCALE).then_inc(wg_hi.sem, 1)
            act.wait_ge(pad_done.sem, 1)

            def normalise(n, src, dst):
                for j in range(GB):
                    ins = act.activation(dst[:, j, :], src[:, j, :], ACT.Identity, bias=lnm[:, n, j:j + 1],
                                         scale=lnr[:, n, j:j + 1])
                return ins

            def do_a(step, g):
                name, t, c = named(step)
                if name == "ln1":
                    act.wait_ge(ln1_ready.sem, ln1_ready.at(g))
                    normalise(0, xin, xn1).then_inc(xn1_done.sem, 1)
                elif name == "xn1t":
                    act.wait_ge(xn1t_ps.sem, xn1t_ps.at(g))
                    act.activation(xn1t[:, :], pa[:, 0, :], ACT.Copy).then_inc(xn1t_done.sem, 1)
                elif name == "qkv":
                    act.wait_ge(qb_done.sem, qb_done.at(g))
                    act.activation(qsq[:, :, :], qb[:, :, :], ACT.Square).then_inc(qk_sq.sem, 1)
                    act.wait_ge(kb_done.sem, kb_done.at(g))
                    act.activation(ksq[0:SC, :, :], kb[0:SC, :, :], ACT.Square).then_inc(qk_sq.sem, 1)
                elif name == "rms_k":
                    act.wait_ge(kf_done.sem, kf_done.at(g))
                    act.activation(k_hi[0:SC, :, :], kb[0:SC, :, :], ACT.Copy).then_inc(kh_done.sem, 1)
                elif name == "rms_q":
                    act.wait_ge(q_hi_done.sem, q_hi_done.at(g))
                    act.activation(q_st[:, :, :, 0:HD], q_hi[:, :, :].rearrange("p t (h d) -> p t h d", h=H),
                                   ACT.Copy).then_inc(first_done.sem, 1)
                    act.wait_ge(kh_done.sem, kh_done.at(g))
                    act.activation(k_st[0:SC, :, :, 0:HD], k_hi[0:SC, :, :].rearrange("p t (h d) -> p t h d", h=H),
                                   ACT.Copy).then_inc(first_done.sem, 1)
                elif name == "qkht":
                    act.wait_ge(qkht_ps.sem, qkht_ps.at(g))
                    act.activation(qkht[:, :], pa16[:, 0:GB * (S + SC)], ACT.Copy).then_inc(qkht_done.sem, 1)
                elif name == "stacks":
                    act.wait_ge(st_ps.sem, st_ps.at(g, t + 1))
                    act.activation(st_t[:, :], pm16[:, 0:NQ * (S + SC)], ACT.Copy).then_inc(st_done.sem, 1)
                elif name == "scores":
                    act.wait_ge(s_ps.sem, s_ps.at(g, 2 * t + c + 1))
                    for i in (2 * c, 2 * c + 1):
                        act.activation(probs[0:SC, i, :, :], pa[0:SC, i % 2, :], ACT.Exp).then_inc(p_done.sem, 1)
                elif name == "values" and c == 1:
                    act.wait_ge(o_ps.sem, o_ps.at(g, t + 1))
                    act.activation(o_t[:, :], pa[:, BO, :], ACT.Copy).then_inc(o_done.sem, 1)
                elif name == "ont":
                    act.wait_ge(ont_ps.sem, ont_ps.at(g))
                    act.activation(on_t[:, :], pa[:, BM, :], ACT.Copy).then_inc(ont_done.sem, 1)

            def do_b(step, g):
                name, t, c = named(step)
                if name == "ln2":
                    act.wait_ge(ln2_ready.sem, ln2_ready.at(g))
                    normalise(1, x1, xn2).then_inc(xn2_done.sem, 1)
                elif name == "ln3":
                    act.wait_ge(ln_ready.sem, ln_ready.at(g, 1))
                    normalise(2, x2, xn3).then_inc(xn3_done.sem, 1)
                elif name == "ln4":
                    act.wait_ge(ln_ready.sem, ln_ready.at(g, 2))
                    normalise(2, x3, xn4).then_inc(xn4_done.sem, 1)
                elif name == "quant":
                    act.wait_ge(sc1_done.sem, sc1_done.at(g))
                    for j in range(GB):
                        ins = act.activation(xr[:, j, :], xn2[:, j, :], ACT.Identity, bias=magic[:, 0:1],
                                             scale=sc1[:, j:j + 1])
                    ins.then_inc(xr_done.sem, 1)
                    for j in range(GB):
                        ins = act.activation(dg[:, j, :], id_f[:, :], ACT.Copy, scale=inv1[:, j:j + 1])
                    ins.then_inc(dg_done.sem, 1)
                elif name == "xit":
                    act.wait_ge(xit_ps.sem, xit_ps.at(g))
                    act.activation(xi_t[:, :], pb[:, :], ACT.Identity, bias=unmagic[:, 0:1]).then_inc(xit_done.sem, 1)
                elif name == "sbc":
                    act.wait_ge(sbc_ps.sem, sbc_ps.at(g))
                    act.activation(sbc[:, :, :], pb[:, :], ACT.Copy).then_inc(sbc_done.sem, 1)
                elif name == "fc1":
                    act.wait_ge(hs_done.sem, hs_done.at(g, t + 1))
                    act.activation(cv[:, t % 2, :, :], hs[:, t % 2, :, 1:S + 1], ACT.Identity,
                                   bias=cb_s[:, t:t + 1], scale=cw_s[:, t, 1:2]).then_inc(mid_done.sem, 1)
                elif name == "taps":
                    act.wait_ge(cv_done.sem, cv_done.at(g, t + 1))
                    act.activation(th[:, t % 2, :], cv2[:, t % 2, :, :], ACT.Tanh, scale=0.5).then_inc(th_done.sem, 1)
                elif name == "h2t":
                    act.wait_ge(sc2_done.sem, sc2_done.at(g, t + 1))
                    act.activation(hr[:, t % 2, :], pb[:, :], ACT.Identity, bias=magic[:, 0:1],
                                   scale=sc2[:, t:t + 1]).then_inc(hr_done.sem, 1)
                elif name == "hit":
                    act.wait_ge(hit_ps.sem, hit_ps.at(g, t + 1))
                    act.activation(hi_t[:, t, :, :], pb[:, :], ACT.Identity, bias=unmagic[:, 0:1])\
                       .then_inc(hit_done.sem, 1)
                elif name == "xn3t":
                    act.wait_ge(xn3t_ps.sem, xn3t_ps.at(g))
                    act.activation(xn3t[:, :], pb[:, :], ACT.Copy).then_inc(xn3t_done.sem, 1)
                elif name == "bf":
                    act.wait_ge(bf_ps.sem, bf_ps.at(g))
                    act.activation(bft[:, :], pb[:, :], ACT.Identity, bias=aw1b_s[:, 0:1]).then_inc(bf_done.sem, 1)
                elif name == "s1":
                    act.wait_ge(nmax1_done.sem, nmax1_done.at(g))
                    for j in range(GB):
                        ins = act.activation(p1[:, j, :], pb[:, j * SC:(j + 1) * SC], ACT.Exp, bias=nmax1[:, j:j + 1],
                                             scale=D ** -0.5, accum_out=l1[:, j:j + 1])
                    ins.then_inc(p1_done.sem, 1)
                elif name == "p1t":
                    act.wait_ge(p1t_ps.sem, p1t_ps.at(g))
                    act.activation(p1t[0:SC, :], pb[0:SC, :], ACT.Copy).then_inc(p1t_done.sem, 1)
                elif name == "oc":
                    act.wait_ge(oc_ps.sem, oc_ps.at(g))
                    act.activation(oct_[:, :], pb[:, :], ACT.Copy).then_inc(oc_done.sem, 1)
                elif name == "xn4t":
                    act.wait_ge(xn4t_ps.sem, xn4t_ps.at(g))
                    act.activation(x4h[:, :], pb[:, :], ACT.Copy).then_inc(x4h_done.sem, 1)
                elif name == "gate":
                    act.wait_ge(gsub_done.sem, gsub_done.at(g))
                    act.activation(gexp[:, :, :], gsub[:, :, :], ACT.Exp, scale=1.0 / WSCALE).then_inc(gexp_done.sem, 1)

            def do_c(part, g):
                what, u = part
                if what == "g":
                    act.wait_ge(g_ps.sem, g_ps.at(g, u + 1))
                    act.activation(tg[:, u % 2, :], pg[:, :], ACT.Tanh, scale=0.5 / WSCALE).then_inc(tg_done.sem, 1)

                if what == "d" and u % 2 and u // 2 in SIDE:
                    e = u // 2
                    act.wait_ge(d_ps.sem, d_ps.at(g, e + 1))
                    if e == SIDE[0]:
                        act.wait_ge(aff_done.sem, aff_done.at(g))
                    if nth(e) == 3:
                        act.wait_ge(sum_done.sem, sum_done.at(g, 1))
                    for j in range(GB):
                        ins = act.activation(side[:, nth(e) % 2, j, :], py[:, j, :], ACT.Copy, scale=aff[:, j, e:e + 1])
                    ins.then_inc(side_done.sem, 1)
                if what == "u":
                    act.wait_ge(u_ps.sem, u_ps.at(g, u + 1))
                    act.activation(us[:, u % 3, :], pu[:, :], ACT.Copy, scale=0.5 / WSCALE ** 2).then_inc(us_done.sem, 1)

            periods(act, lambda n, a, b, d, c: run_turns("act", n, a, b, d, c, do_a, do_b, do_c))

        @block.gpsimd
        def _(pool):
            for tile, value in ((ones[:, :], 1.0), (magic[:, :], MAGIC), (unmagic[:, :], -MAGIC), (q_st[:, :, :, :], 0.0),
                                (ms[:, :, :], 0.0), (k_st[:, :, :, :], 0.0), (v_st[:, :, :, :], 1.0), (hs[:, :, :, :], 0.0)):
                ins = pool.memset(tile, value)
            ins.then_inc(pad_done.sem, 1)
            pool.wait_ge(pad_done.sem, 1)
            pool.memset(k_st[:, :, :, 3 * HD:3 * HD + 1], 1.0)
            pool.wait_ge(setup_done.sem, 1)

            def do_a(step, g):
                name, t, c = named(step)
                if name == "xn1t":
                    pool.wait_ge(xres_in.sem, xres_in.at(g, 16))
                    if later(g):
                        pool.wait_ge(x1_done.sem, x1_done.at(g - 1))
                    pool.tensor_tensor(xres_b[:, :, :], xres[:, :, :], bp_s[:, :].unsqueeze(1).broadcast_to([128, GB, D]),
                                       ALU.add).then_inc(xres_b_done.sem, 1)
                elif name == "rms_q":
                    pool.wait_ge(q_hi_done.sem, q_hi_done.at(g))
                    one = ones[:, :].rearrange("p (h d) -> p h d", h=H).unsqueeze(1).broadcast_to([128, GB, H, HD])
                    pool.tensor_tensor(q_st[:, :, :, 2 * HD:3 * HD], split_head(q_hi[:, :, :]), one, ALU.mult).then_inc(dup_done.sem, 1)
                    pool.wait_ge(kh_done.sem, kh_done.at(g))
                    pool.tensor_tensor(k_st[0:SC, :, :, HD:2 * HD], split_head(k_hi[0:SC, :, :]), one[0:SC], ALU.mult).then_inc(dup_done.sem, 1)
                elif name == "qkht":
                    pool.wait_ge(qkht_done.sem, qkht_done.at(g))
                    for j in range(GB):
                        k0 = GB * S + j * SC
                        pool.tensor_tensor(kbd[:, j, :, :],
                                           qkht[:, k0:k0 + SC].unsqueeze(1).broadcast_to([128, H, SC]),
                                           mask_h[:, :].unsqueeze(2).broadcast_to([128, H, SC]), ALU.mult)\
                            .then_inc(kbd_done.sem, 1)

            def do_c(part, g):
                what, u = part
                if what == "u":
                    pool.wait_ge(gw_done.sem, gw_done.at(g, u + 1))
                    pool.wait_ge(us_done.sem, us_done.at(g, u + 1))
                    pool.tensor_tensor(hu[:, u % 3, :], gw[:, u % 3, :], us[:, u % 3, :], ALU.mult)\
                        .then_inc(hu_done.sem, 1)
                elif what == "d" and u % 2 and nth(u // 2) > 1 and u // 2 in SIDE:
                    n = nth(u // 2)
                    if n == 2 and later(g):
                        pool.wait_ge(out_done.sem, out_done.at(g - 1, 16))
                    pool.wait_ge(side_done.sem, side_done.at(g, n))
                    if n == 3:
                        pool.wait_ge(sum_done.sem, sum_done.at(g, 1))
                    pool.tensor_tensor(acc2[:, :, :], side[:, 1, :, :] if n == 2 else acc2[:, :, :],
                                       side[:, n % 2, :, :], ALU.add).then_inc(sum_done.sem, 1)
                elif what == "d" and u == NU - 1:
                    pool.wait_ge(sum_done.sem, sum_done.at(g, 2))
                    pool.wait_ge(comb_done.sem, comb_done.at(g, nth(E - 1)))
                    pool.tensor_tensor(acc2[:, :, :], acc2[:, :, :], acc[:, :, :], ALU.add).then_inc(sum_done.sem, 1)

            def do_b(step, g):
                name, t, c = named(step)
                if name == "fc2":
                    pool.wait_ge(x2_done.sem, x2_done.at(g))
                    pool.tensor_tensor(x2b[:, :, :], x2[:, :, :], a2b_s[:, :].unsqueeze(1).broadcast_to([128, GB, D]),
                                       ALU.add).then_inc(x2b_done.sem, 1)

            periods(pool, lambda n, a, b, d, c: run_turns("pool", n, a, b, d, c, do_a, do_b, do_c))

        @block.vector
        def _(dve):
            class Chain:

                def __init__(self, sig):
                    self.sig, self.g, self.k = sig, 0, 0

                def start(self, g):
                    self.g, self.k = g, 0

                def link(self, ins):
                    self.k += 1
                    ins.then_inc(self.sig.sem, 1)
                    dve.wait_ge(self.sig.sem, self.sig.at(self.g, self.k))

                def end(self):
                    if self.k != self.sig.per:
                        raise ValueError(f"{self.k} links")

            cn, ca, cb, cd, cs = Chain(link_n), Chain(link_a), Chain(link_b), Chain(link_d), Chain(link_s)

            def rsqrt(chain, y, v, root, r):
                chain.link(dve.tensor_scalar(y.bitcast(I32), v.bitcast(I32), -0.5, RSQRT_SEED, ALU.mult, ALU.add))
                chain.link(dve.tensor_tensor(root, v, y, ALU.mult))
                for last in (False, False, True):
                    chain.link(dve.scalar_tensor_tensor(out=r, in0=root, scalar=-0.5, in1=y, op0=ALU.mult, op1=ALU.mult))
                    if not last:
                        dve.scalar_tensor_tensor(out=root, in0=r, scalar=1.5, in1=root, op0=ALU.add, op1=ALU.mult)
                    ins = dve.scalar_tensor_tensor(out=y, in0=r, scalar=1.5, in1=y, op0=ALU.add, op1=ALU.mult)
                    if not last:
                        chain.link(ins)
                return ins

            def layernorm(chain, n, src):
                for j in range(GB):
                    ins = dve.bn_stats(stats[:, n, j, :], src[:, j, :])
                chain.link(ins)
                dve.tensor_copy(lnv[:, n, 0:1], stats[:, n, 0, 1:2])
                for j in range(GB):
                    ins = dve.bn_aggr(mv[:, n, j, :], stats[:, n, j, :])
                chain.link(ins)
                chain.link(dve.tensor_scalar(lnv[:, n, :], mv[:, n, :, 1], EPS_LN, None, ALU.add))
                chain.link(rsqrt(chain, lnr[:, n, :], lnv[:, n, :], lnd[:, n, :], lnt[:, n, :]))
                return dve.scalar_tensor_tensor(out=lnm[:, n, :], in0=mv[:, n, :, 0], scalar=-1.0, in1=lnr[:, n, :],
                                                op0=ALU.mult, op1=ALU.mult)

            for bank in (pa[:, :, :], pb[:, :], pg[:, :], pu[:, :], py[:, :, :]):
                dve.memset(bank, 0.0)
            dve.wait_ge(small_in.sem, 16 * 22)
            dve.wait_ge(pad_done.sem, 1)
            dve.tensor_copy(id_h[:, :], id_f[:, :])
            dve.tensor_copy(mask_h[:, :], mask_f[:, :])
            cs.link(dve.tensor_tensor(gg_s[:, :], gq_s[:, :], gk_s[:, :], ALU.mult))
            cs.link(dve.tensor_scalar(gg_s[:, :], gg_s[:, :], HD ** -0.5, None, ALU.mult))
            dve.tensor_reduce(wabs[:, 0:1], w1_f, AX.X, ALU.add, apply_absolute_value=True)
            dve.tensor_reduce(wabs[:, 1:2], w2_f, AX.XY, ALU.add, apply_absolute_value=True)\
               .then_inc(wabs_done.sem, 1)
            dve.wait_ge(wsum_done.sem, 1)
            cs.link(dve.tensor_scalar(wmean[:, :], pb[:, 0:2], 1.0 / (D * HID), CLIP, ALU.mult, ALU.max))
            cs.link(dve.reciprocal(winv[:, :], wmean[:, :]))
            for w, w_int, n in ((w1_f, w1_i[:, :], 0), (w2_f, w2_i[:, :, :], 1)):
                cs.link(dve.tensor_scalar(w, w, winv[:, n:n + 1], MAGIC, ALU.mult, ALU.add))
                cs.link(dve.tensor_scalar(w, w, MAGIC, 1.0, ALU.subtract, ALU.min))
                cs.link(dve.tensor_scalar(w_int, w, -1.0, None, ALU.max))
            for n, (w, lo, hi) in enumerate(((w_stage, wg_l, wg_h), (w_stage, wu_l, wu_h))):
                dve.wait_ge(wg_hi.sem, n + 1)
                if n == 0:
                    cs.link(dve.scalar_tensor_tensor(out=gate_l[:, :], in0=gate_f[:, :], scalar=WSCALE, in1=gate_h[:, :],
                                                     op0=ALU.mult, op1=ALU.subtract))
                ins = dve.scalar_tensor_tensor(out=lo[:, :], in0=w, scalar=WSCALE, in1=hi[:, :],
                                               op0=ALU.mult, op1=ALU.subtract)
                if n == 0:
                    ins.then_inc(wg_used.sem, 1)
            ins.then_inc(setup_done.sem, 1)
            dve.wait_ge(setup_done.sem, 1)

            def do_a(step, g):
                name, t, c = named(step)
                if name == "ln1":
                    dve.wait_ge(xin_in.sem, xin_in.at(g, 16))
                    layernorm(cn, 0, xin).then_inc(ln1_ready.sem, 1)
                elif name == "qkv":
                    dve.wait_ge(q_ps.sem, q_ps.at(g))
                    dve.tensor_tensor(qb[:, :, :], pa[:, 1, :].rearrange("p (t d) -> p t d", t=GB),
                                      bq_s[:, :].unsqueeze(1).broadcast_to([128, GB, D]), ALU.add)\
                       .then_inc(qb_done.sem, 1)
                    dve.wait_ge(k_ps.sem, k_ps.at(g))
                    dve.tensor_tensor(kb[0:SC, :, :], pa[0:SC, 2, :].rearrange("p (t d) -> p t d", t=GB),
                                      bk_s[0:SC, :].unsqueeze(1).broadcast_to([SC, GB, D]), ALU.add)\
                       .then_inc(kb_done.sem, 1)
                    dve.wait_ge(v_ps.sem, v_ps.at(g))
                    for j in range(GB):
                        ins = dve.tensor_tensor(v_st[0:SC, j, :, 0:HD],
                                                pa[0:SC, BO, j * D:(j + 1) * D].rearrange("p (h d) -> p h d", h=H),
                                                bv_s[0:SC, :].rearrange("p (h d) -> p h d", h=H), ALU.add)
                    ins.then_inc(v_done.sem, 1)
                elif name == "rms":
                    dve.wait_ge(qk_sq.sem, qk_sq.at(g, 1))
                    dve.tensor_reduce(ms[:, 0, :], qsq[:, :, :].rearrange("p t (h d) -> p (t h) d", h=H), AX.X, ALU.add)
                    dve.wait_ge(qk_sq.sem, qk_sq.at(g, 2))
                    ca.link(dve.tensor_reduce(ms[0:SC, 1, :], ksq[0:SC, :, :].rearrange("p t (h d) -> p (t h) d", h=H),
                                              AX.X, ALU.add))
                    ca.link(dve.tensor_scalar(ms[:, :, :], ms[:, :, :], 1.0 / HD, EPS_RMS, ALU.mult, ALU.add))
                    ca.link(rsqrt(ca, rr[:, :, :], ms[:, :, :], root[:, :, :], nt[:, :, :]))
                elif name == "rms_k":
                    rk = rr[0:SC, 1, :].unsqueeze(2).broadcast_to([SC, GB * H, HD])
                    gg = gg_s[0:SC, :].unsqueeze(1).broadcast_to([SC, GB * H, HD])
                    k3 = kb[0:SC, :, :].rearrange("p t (h d) -> p (t h) d", h=H)
                    ca.link(dve.tensor_tensor(k3, k3, rk, ALU.mult))
                    dve.tensor_tensor(k3, k3, gg, ALU.mult).then_inc(kf_done.sem, 1)
                elif name == "rms_q":
                    rq = rr[:, 0, :].unsqueeze(2).broadcast_to([128, GB * H, HD])
                    q3 = qb[:, :, :].rearrange("p t (h d) -> p (t h) d", h=H)
                    ca.link(dve.tensor_tensor(q3, q3, rq, ALU.mult))
                    dve.tensor_copy(q_hi[:, :, :], qb[:, :, :]).then_inc(q_hi_done.sem, 1)
                    dve.wait_ge(kh_done.sem, kh_done.at(g))
                    dve.tensor_tensor(k_st[0:SC, :, :, 2 * HD:3 * HD], split_head(kb[0:SC, :, :]),
                                      split_head(k_hi[0:SC, :, :]), ALU.subtract).then_inc(kl_done.sem, 1)
                    dve.wait_ge(q_hi_done.sem, q_hi_done.at(g))
                    dve.tensor_tensor(q_st[:, :, :, HD:2 * HD], split_head(qb[:, :, :]), split_head(q_hi[:, :, :]),
                                      ALU.subtract).then_inc(ql_done.sem, 1)
                elif name == "max":
                    dve.wait_ge(max_ps.sem, max_ps.at(g, 4 * t + c + 1))
                    dve.tensor_reduce(q_st[:, t, 4 * c:4 * c + 4, 3 * HD],
                                      pa[:, BM, 0:4 * SC].rearrange("p (h k) -> p h k", h=4), AX.X, ALU.max,
                                      negate=True).then_inc(max_done.sem, 1)
                elif name == "turn":
                    dve.wait_ge(oq_ps.sem, oq_ps.at(g, t + 1))
                    oq = pa[:, BO, :].rearrange("p (i n d) -> p i n d", i=HQ, d=32)
                    ca.link(dve.reciprocal(rden[:, :, :], oq[:, :, :, HD]))
                    dve.tensor_tensor(o_n[:, t, :].rearrange("p (n i d) -> p i n d", n=NQ, d=HD), oq[:, :, :, 0:HD],
                                      rden[:, :, :].unsqueeze(3).broadcast_to([128, HQ, NQ, HD]), ALU.mult)\
                       .then_inc(on_done.sem, 1)
                elif name == "proj":
                    dve.wait_ge(y_ps.sem, y_ps.at(g))
                    dve.wait_ge(xres_b_done.sem, xres_b_done.at(g))
                    if later(g):
                        dve.wait_ge(x2_done.sem, x2_done.at(g - 1))
                    dve.tensor_tensor(x1[:, :, :], pa[:, BO, :].rearrange("p (t d) -> p t d", t=GB), xres_b[:, :, :],
                                      ALU.add).then_inc(x1_done.sem, 1)

            def do_b(step, g):
                name, t, c = named(step)
                if name == "ln2":
                    dve.wait_ge(x1_done.sem, x1_done.at(g))
                    layernorm(cb, 1, x1).then_inc(ln2_ready.sem, 1)
                elif name == "quant":
                    dve.wait_ge(xn2_done.sem, xn2_done.at(g))
                    cb.link(dve.tensor_reduce(am1[:, :], xn2[:, :, :], AX.X, ALU.max, apply_absolute_value=True))
                    cb.link(dve.tensor_scalar(am1[:, :], am1[:, :], CLIP, None, ALU.max))
                    cb.link(dve.reciprocal(sc1[:, :], am1[:, :]))
                    dve.tensor_scalar(inv1[:, :], am1[:, :], wmean[:, 0:1], 1.0 / 127.0, ALU.mult, ALU.mult)
                    dve.tensor_scalar(sc1[:, :], sc1[:, :], 127.0, None, ALU.mult).then_inc(sc1_done.sem, 1)
                elif name == "fc1":
                    dve.wait_ge(fc1_ps.sem, fc1_ps.at(g, t + 1))
                    if t == 0:
                        dve.wait_ge(sbc_done.sem, sbc_done.at(g))
                    dve.tensor_tensor(hs[:, t % 2, :, 1:S + 1], pb[:, :].rearrange("p (t s) -> p t s", t=GB),
                                      sbc[:, :, :], ALU.mult).then_inc(hs_done.sem, 1)
                elif name == "taps":
                    dve.wait_ge(hs_done.sem, hs_done.at(g, t + 1))
                    dve.wait_ge(mid_done.sem, mid_done.at(g, t + 1))
                    cb.link(dve.scalar_tensor_tensor(out=cv1[:, :, :], in0=hs[:, t % 2, :, 0:S], scalar=cw_s[:, t, 0:1],
                                                     in1=cv[:, t % 2, :, :], op0=ALU.mult, op1=ALU.add))
                    dve.scalar_tensor_tensor(out=cv2[:, t % 2, :, :], in0=hs[:, t % 2, :, 2:S + 2],
                                             scalar=cw_s[:, t, 2:3], in1=cv1[:, :, :], op0=ALU.mult, op1=ALU.add)\
                       .then_inc(cv_done.sem, 1)
                elif name == "silu":
                    dve.wait_ge(cv_done.sem, cv_done.at(g, t + 1))
                    dve.wait_ge(th_done.sem, th_done.at(g, t + 1))
                    dve.scalar_tensor_tensor(out=h2[:, t, :], in0=th[:, t % 2, :], scalar=1.0,
                                             in1=cv2[:, t % 2, :, :].rearrange("p t s -> p (t s)"),
                                             op0=ALU.add, op1=ALU.mult).then_inc(h2_done.sem, 1)
                elif name == "h2t":
                    dve.wait_ge(h2t_ps.sem, h2t_ps.at(g, t + 1))
                    a, s = am2[:, t:t + 1], sc2[:, t:t + 1]
                    cb.link(dve.tensor_reduce(a, pb[:, :], AX.X, ALU.max, apply_absolute_value=True))
                    cb.link(dve.tensor_scalar(a, a, 0.5, CLIP, ALU.mult, ALU.max))
                    cb.link(dve.reciprocal(s, a))
                    dve.tensor_scalar(s, s, 0.5 * 127.0, None, ALU.mult).then_inc(sc2_done.sem, 1)
                elif name == "fc2":
                    cb.link(dve.tensor_scalar(inv2[:, :], am2[:, :], wmean[:, 1:2], 1.0 / 127.0, ALU.mult, ALU.mult))
                    dve.wait_ge(fc2_ps.sem, fc2_ps.at(g))
                    if later(g):
                        dve.wait_ge(xn3_done.sem, xn3_done.at(g - 1))
                        dve.wait_ge(x2b_done.sem, x2b_done.at(g - 1))
                    for j in range(GB):
                        ins = dve.scalar_tensor_tensor(out=x2[:, j, :], in0=pb[:, j * D:(j + 1) * D],
                                                       scalar=inv2[:, j:j + 1], in1=x1[:, j, :],
                                                       op0=ALU.mult, op1=ALU.add)
                    ins.then_inc(x2_done.sem, 1)
                elif name == "ln3":
                    dve.wait_ge(x2_done.sem, x2_done.at(g))
                    layernorm(cd, 2, x2).then_inc(ln_ready.sem, 1)
                elif name == "s1":
                    dve.wait_ge(s1_ps.sem, s1_ps.at(g))
                    cd.link(dve.tensor_reduce(nmax1[:, :], pb[:, 0:GB * SC].rearrange("p (t k) -> p t k", t=GB), AX.X,
                                              ALU.max, negate=True))
                    dve.tensor_scalar(nmax1[:, :], nmax1[:, :], D ** -0.5, None, ALU.mult).then_inc(nmax1_done.sem, 1)
                elif name == "p1n":
                    dve.wait_ge(p1_done.sem, p1_done.at(g))
                    cd.link(dve.reciprocal(rl1[:, :], l1[:, :]))
                    dve.tensor_tensor(p1n[:, :, :], p1[:, :, :], rl1[:, :].unsqueeze(2).broadcast_to([128, GB, SC]),
                                      ALU.mult).then_inc(p1n_done.sem, 1)
                elif name == "fused":
                    dve.wait_ge(fu_ps.sem, fu_ps.at(g))
                    dve.wait_ge(x2b_done.sem, x2b_done.at(g))
                    dve.tensor_tensor(x3[:, :, :], pb[:, :].rearrange("p (t d) -> p t d", t=GB), x2b[:, :, :],
                                      ALU.add).then_inc(x3_done.sem, 1)
                elif name == "ln4":
                    dve.wait_ge(x3_done.sem, x3_done.at(g))
                    layernorm(cd, 2, x3).then_inc(ln_ready.sem, 1)
                elif name == "xn4t":
                    dve.wait_ge(xn4t_ps.sem, xn4t_ps.at(g))
                    dve.wait_ge(x4h_done.sem, x4h_done.at(g))
                    dve.tensor_tensor(x4l[:, :], pb[:, :], x4h[:, :], ALU.subtract).then_inc(x4l_done.sem, 1)
                elif name == "gate":
                    dve.wait_ge(lg_ps.sem, lg_ps.at(g))
                    lg = pb[:, 0:GB * E].rearrange("p (t e) -> p t e", t=GB)
                    cd.link(dve.tensor_reduce(gmax[:, :], lg, AX.X, ALU.max))
                    dve.tensor_tensor(gsub[:, :, :], lg, gmax[:, :].unsqueeze(2).broadcast_to([128, GB, E]),
                                      ALU.subtract).then_inc(gsub_done.sem, 1)
                    dve.wait_ge(gexp_done.sem, gexp_done.at(g))
                    cd.link(dve.tensor_reduce(gsum[:, :], gexp[:, :, :], AX.X, ALU.add))
                    cd.link(dve.reciprocal(gsum[:, :], gsum[:, :]))
                    dve.tensor_tensor(aff[:, :, :], gexp[:, :, :], gsum[:, :].unsqueeze(2).broadcast_to([128, GB, E]),
                                      ALU.mult).then_inc(aff_done.sem, 1)

            def do_c(part, g):
                what, u = part
                if what == "u":
                    dve.wait_ge(tg_done.sem, tg_done.at(g, u + 1))
                    dve.scalar_tensor_tensor(out=gw[:, u % 3, :], in0=tg[:, u % 2, :], scalar=1.0, in1=pg[:, :],
                                             op0=ALU.add, op1=ALU.mult).then_inc(gw_done.sem, 1)
                elif what == "d" and u % 2 and u // 2 not in SIDE:
                    e = u // 2
                    dve.wait_ge(d_ps.sem, d_ps.at(g, e + 1))
                    if e:
                        dve.wait_ge(comb_done.sem, comb_done.at(g, nth(e) - 1))
                    else:
                        dve.wait_ge(aff_done.sem, aff_done.at(g))
                        if later(g):
                            dve.wait_ge(sum_done.sem, sum_done.at(g - 1, len(SIDE)))
                    before = acc if e else x3
                    for j in range(GB):
                        ins = dve.scalar_tensor_tensor(out=acc[:, j, :], in0=py[:, j, :], scalar=aff[:, j, e:e + 1],
                                                       in1=before[:, j, :], op0=ALU.mult, op1=ALU.add)
                    ins.then_inc(comb_done.sem, 1)

            def body(n, a, b, d, c):
                for chain, g in ((cn, n), (ca, a), (cb, b), (cd, d)):
                    if g is not None:
                        chain.start(g)
                run_turns("dve", n, a, b, d, c, do_a, do_b, do_c)
                for chain, g in ((cn, n), (ca, a), (cb, b), (cd, d)):
                    if g is not None:
                        chain.end()

            periods(dve, body)


def kernel(x, ctx_1024, L0_xattn_Wq, L0_xattn_bq, L0_xattn_Wkv, L0_xattn_bkv, L0_xattn_Wproj, L0_xattn_bproj,
           L0_xattn_gq, L0_xattn_gk, L0_ffn_w1, L0_ffn_conv_w, L0_ffn_conv_b, L0_ffn_w2, L1_xattn_w1_w,
           L1_xattn_w1_b, L1_xattn_w2_w, L1_xattn_w2_b, L1_ffn_gate_w, L1_ffn_Wg, L1_ffn_Wu, L1_ffn_Wd):
    import numpy as np
    import concourse.bacc as bacc
    from concourse.bass_utils import run_bass_kernel_spmd

    def a(v):
        return np.asarray(v)

    arrays = {
        "x": a(x), "ctx": a(ctx_1024), "ctx_t": a(ctx_1024).transpose(0, 2, 1),
        "wq": a(L0_xattn_Wq), "bq": a(L0_xattn_bq), "wkv": a(L0_xattn_Wkv), "bkv": a(L0_xattn_bkv),
        "wproj": a(L0_xattn_Wproj), "bproj": a(L0_xattn_bproj), "gq": a(L0_xattn_gq), "gk": a(L0_xattn_gk),
        "w1t": a(L0_ffn_w1).T,
        "conv_w": a(L0_ffn_conv_w).reshape(KB, 128, 3).transpose(1, 0, 2),
        "conv_b": a(L0_ffn_conv_b).reshape(KB, 128).T,
        "w2t": a(L0_ffn_w2).T.reshape(KB, 128, D).transpose(1, 0, 2),
        "aw1t": a(L1_xattn_w1_w).T, "aw1b": a(L1_xattn_w1_b).reshape(D, 1),
        "aw2t": a(L1_xattn_w2_w).T.reshape(2, D, D).transpose(1, 0, 2), "aw2b": a(L1_xattn_w2_b),
        "gate": a(L1_ffn_gate_w),
        "wg": a(L1_ffn_Wg).transpose(1, 0, 2).reshape(D, E * I),
        "wu": a(L1_ffn_Wu).transpose(1, 0, 2).reshape(D, E * I),
        "wd": a(L1_ffn_Wd).reshape(NU, 128, D).transpose(1, 0, 2),
        "ident": np.eye(128, dtype=np.float32),
        "head_mask": np.repeat(np.eye(H, dtype=np.float32), HD, axis=0),
    }
    nc = bacc.Bacc("TRN2", target_bir_lowering=False, num_devices=1)
    arrays = {f"in_{n}": np.ascontiguousarray(v) for n, v in arrays.items()}
    args = [nc.dram_tensor(n, v.shape, mybir.dt.from_np(v.dtype), kind="ExternalInput").ap() for n, v in arrays.items()]
    result = nc.dram_tensor("out_x", (B, S, D), F32, kind="ExternalOutput").ap()
    build_program(nc, *args, result)
    r = run_bass_kernel_spmd(nc, [arrays], core_ids=[0])
    return r.results[0]["out_x"]
```
